# Optimizing a Trainium2 kernel written in Bass

```python
import numpy as np
import jax
import jax.numpy as jnp

def _softmax(x, axis=-1):
    return jax.nn.softmax(x, axis=axis)
def _gelu(x):
    return jax.nn.gelu(x, approximate=True)
def _silu(x):
    return jax.nn.silu(x)
def _sigmoid(x):
    return jax.nn.sigmoid(x)
def _layernorm(x, axis=-1, eps=1e-5):
    m = jnp.mean(x, axis=axis, keepdims=True)
    v = jnp.var(x, axis=axis, keepdims=True)
    return (x - m) / jnp.sqrt(v + eps)
def _scatter_add(tgt, idx, src, axis=0):
    return tgt.at[idx].add(src)
def _segment_sum(src, seg, n):
    return jax.ops.segment_sum(src, seg, n)

kernel_name = 'mk_conv_preact_d4_conv_nchw48_744282'

def setup_inputs(seed: int = 0):
    np.random.seed(seed)
    _w = jnp.asarray
    def _rec_inputs():
        import jax
        import jax.numpy as jnp
        _gk = jax.random.key(seed)
        x = -0.0004039 + 1 * jax.random.normal(jax.random.fold_in(_gk, 1), (4, 48, 256, 256), jnp.float32)
        return x
    x = _rec_inputs()
    def _L0_conv_setup():
        import jax, jax.numpy as jnp
        import numpy as np
        from jax import lax
        NUM_HEADS = 1
        DN = ('NCHW', 'OIHW', 'NCHW')
        EPS = 1e-12

        def _l2_normalize(t):
            n = jnp.sqrt(jnp.sum(t * t, axis=-1, keepdims=True))
            return t / jnp.maximum(n, EPS)
        key = jax.random.key(seed)
        k0, k1, k2, k3 = jax.random.split(key, 4)
        b, c, h, w = (4, 48, 256, 256)
        x = jax.random.normal(k0, (b, c, h, w), dtype=jnp.float32)
        qkv_w = jax.random.normal(k1, (3 * c, c, 1, 1), dtype=jnp.float32) * 0.05
        dw_w = jax.random.normal(k2, (3 * c, 1, 3, 3), dtype=jnp.float32) * 0.05
        proj_w = jax.random.normal(k3, (c, c, 1, 1), dtype=jnp.float32) * 0.05
        temperature = jnp.ones((NUM_HEADS, 1, 1), dtype=jnp.float32)
        return {'x': x, 'qkv_w': qkv_w, 'dw_w': dw_w, 'proj_w': proj_w, 'temperature': temperature}
    _L0_conv_all = _L0_conv_setup()
    _L0_conv_in = {k: v for k, v in _L0_conv_all.items() if k in ('qkv_w', 'dw_w', 'proj_w', 'temperature', )}
    del _L0_conv_all

    def _L1_conv_setup():
        import jax, jax.numpy as jnp
        import numpy as np
        B, C, H, W = (32, 48, 64, 128)
        K = 5

        def _conv1d(x, w, b):
            y = jax.lax.conv_general_dilated(x, w, window_strides=(1,), padding=[(2, 2)], dimension_numbers=('NCH', 'OIH', 'NCH'))
            return y + b[None, :, None]
        key = jax.random.key(seed)
        ks = jax.random.split(key, 7)
        s = 0.02
        return {'x': jax.random.normal(ks[0], (B, C, H, W), dtype=jnp.float32), 'down_w': jax.random.normal(ks[1], (C, C, K), dtype=jnp.float32) * s, 'down_b': jax.random.normal(ks[2], (C,), dtype=jnp.float32) * s, 'right_w': jax.random.normal(ks[3], (C, C, K), dtype=jnp.float32) * s, 'right_b': jax.random.normal(ks[4], (C,), dtype=jnp.float32) * s, 'left_w': jax.random.normal(ks[5], (C, C, K), dtype=jnp.float32) * s, 'left_b': jax.random.normal(ks[6], (C,), dtype=jnp.float32) * s}
    _L1_conv_all = _L1_conv_setup()
    _L1_conv_in = {k: v for k, v in _L1_conv_all.items() if k in ('down_w', 'down_b', 'right_w', 'right_b', 'left_w', 'left_b', )}
    del _L1_conv_all

    def _L2_conv_setup():
        import jax, jax.numpy as jnp
        import numpy as np
        PATCH = 8
        EPS = 1e-05

        def _conv2d(x, w, b, groups=1, padding='VALID'):
            y = jax.lax.conv_general_dilated(x, w, window_strides=(1, 1), padding=padding, feature_group_count=groups, dimension_numbers=('NCHW', 'OIHW', 'NCHW'))
            return y + b[None, :, None, None]
        key = jax.random.key(seed)
        ks = jax.random.split(key, 8)
        B, C, H, W = (4, 48, 256, 256)
        C6, C2 = (C * 6, C * 2)
        x = jax.random.normal(ks[0], (B, C, H, W), dtype=jnp.float32)
        w_hidden = jax.random.normal(ks[1], (C6, C, 1, 1), dtype=jnp.float32) * 0.05
        b_hidden = jnp.zeros((C6,), dtype=jnp.float32)
        w_dw = jax.random.normal(ks[2], (C6, 1, 3, 3), dtype=jnp.float32) * 0.05
        b_dw = jnp.zeros((C6,), dtype=jnp.float32)
        gamma = jnp.ones((C2,), dtype=jnp.float32)
        beta = jnp.zeros((C2,), dtype=jnp.float32)
        w_out = jax.random.normal(ks[3], (C, C2, 1, 1), dtype=jnp.float32) * 0.05
        b_out = jnp.zeros((C,), dtype=jnp.float32)
        return {'x': x, 'w_hidden': w_hidden, 'b_hidden': b_hidden, 'w_dw': w_dw, 'b_dw': b_dw, 'gamma': gamma, 'beta': beta, 'w_out': w_out, 'b_out': b_out}
    _L2_conv_all = _L2_conv_setup()
    _L2_conv_in = {k: v for k, v in _L2_conv_all.items() if k in ('w_hidden', 'b_hidden', 'w_dw', 'b_dw', 'gamma', 'beta', 'w_out', 'b_out', )}
    del _L2_conv_all

    def _L3_conv_setup():
        import jax, jax.numpy as jnp
        from jax import lax
        import numpy as np
        DIM = 48
        EXPANSION = 3.0
        P = 8
        HIDDEN = int(DIM * EXPANSION)
        C2 = HIDDEN * 2
        key = jax.random.key(seed)
        k0, k1, k2, k3, k4 = jax.random.split(key, 5)
        x = jax.random.normal(k0, (8, DIM, 256, 256), dtype=jnp.float32)
        w_in = jax.random.normal(k1, (C2, DIM), dtype=jnp.float32) * 0.05
        w_dw = jax.random.normal(k2, (C2, 1, 3, 3), dtype=jnp.float32) * 0.1
        fft_mask = 1.0 + 0.1 * jax.random.normal(k3, (C2, 1, 1, P, P // 2 + 1), dtype=jnp.float32)
        w_out = jax.random.normal(k4, (DIM, HIDDEN), dtype=jnp.float32) * 0.05
        return {'x': x, 'w_in': w_in, 'w_dw': w_dw, 'fft_mask': fft_mask, 'w_out': w_out}
    _L3_conv_all = _L3_conv_setup()
    _L3_conv_in = {k: v for k, v in _L3_conv_all.items() if k in ('w_in', 'w_dw', 'fft_mask', 'w_out', )}
    del _L3_conv_all

    return {
        "x": x,
        "L0_conv_qkv_w": _L0_conv_in["qkv_w"],
        "L0_conv_dw_w": _L0_conv_in["dw_w"],
        "L0_conv_proj_w": _L0_conv_in["proj_w"],
        "L0_conv_temperature": _L0_conv_in["temperature"],
        "L1_conv_down_w": _L1_conv_in["down_w"],
        "L1_conv_down_b": _L1_conv_in["down_b"],
        "L1_conv_right_w": _L1_conv_in["right_w"],
        "L1_conv_right_b": _L1_conv_in["right_b"],
        "L1_conv_left_w": _L1_conv_in["left_w"],
        "L1_conv_left_b": _L1_conv_in["left_b"],
        "L2_conv_w_hidden": _L2_conv_in["w_hidden"],
        "L2_conv_b_hidden": _L2_conv_in["b_hidden"],
        "L2_conv_w_dw": _L2_conv_in["w_dw"],
        "L2_conv_b_dw": _L2_conv_in["b_dw"],
        "L2_conv_gamma": _L2_conv_in["gamma"],
        "L2_conv_beta": _L2_conv_in["beta"],
        "L2_conv_w_out": _L2_conv_in["w_out"],
        "L2_conv_b_out": _L2_conv_in["b_out"],
        "L3_conv_w_in": _L3_conv_in["w_in"],
        "L3_conv_w_dw": _L3_conv_in["w_dw"],
        "L3_conv_fft_mask": _L3_conv_in["fft_mask"],
        "L3_conv_w_out": _L3_conv_in["w_out"],
    }

def reference(x, L0_conv_qkv_w, L0_conv_dw_w, L0_conv_proj_w, L0_conv_temperature, L1_conv_down_w, L1_conv_down_b, L1_conv_right_w, L1_conv_right_b, L1_conv_left_w, L1_conv_left_b, L2_conv_w_hidden, L2_conv_b_hidden, L2_conv_w_dw, L2_conv_b_dw, L2_conv_gamma, L2_conv_beta, L2_conv_w_out, L2_conv_b_out, L3_conv_w_in, L3_conv_w_dw, L3_conv_fft_mask, L3_conv_w_out):
    import jax
    import jax.numpy as jnp
    def _L0_conv_ref(x, qkv_w, dw_w, proj_w, temperature):
        import jax, jax.numpy as jnp
        import numpy as np
        from jax import lax
        NUM_HEADS = 1
        DN = ('NCHW', 'OIHW', 'NCHW')
        EPS = 1e-12

        def _l2_normalize(t):
            n = jnp.sqrt(jnp.sum(t * t, axis=-1, keepdims=True))
            return t / jnp.maximum(n, EPS)
        b, c, h, w = x.shape
        heads = NUM_HEADS
        qkv = lax.conv_general_dilated(x, qkv_w, (1, 1), 'VALID', dimension_numbers=DN)
        qkv = lax.conv_general_dilated(qkv, dw_w, (1, 1), ((1, 1), (1, 1)), feature_group_count=3 * c, dimension_numbers=DN)
        q, k, v = jnp.split(qkv, 3, axis=1)
        q = q.reshape(b, heads, c // heads, h * w)
        k = k.reshape(b, heads, c // heads, h * w)
        v = v.reshape(b, heads, c // heads, h * w)
        q = _l2_normalize(q)
        k = _l2_normalize(k)
        attn = jax.nn.softmax(jnp.einsum('bhcn,bhdn->bhcd', q, k) * temperature, axis=-1)
        out = jnp.einsum('bhcd,bhdn->bhcn', attn, v).reshape(b, c, h, w)
        return lax.conv_general_dilated(out, proj_w, (1, 1), 'VALID', dimension_numbers=DN)

    def _L1_conv_ref(x, down_w, down_b, right_w, right_b, left_w, left_b):
        import jax, jax.numpy as jnp
        import numpy as np
        B, C, H, W = (32, 48, 64, 128)
        K = 5

        def _conv1d(x, w, b):
            y = jax.lax.conv_general_dilated(x, w, window_strides=(1,), padding=[(2, 2)], dimension_numbers=('NCH', 'OIH', 'NCH'))
            return y + b[None, :, None]
        Bb, Cc, Hh, Ww = x.shape

        def step(w, b):

            def f(carry, inp):
                nxt = inp + _conv1d(carry, w, b)
                return (nxt, nxt)
            return f
        xs = jnp.moveaxis(x, 2, 0)
        d0 = xs[0]
        _, d_rest = jax.lax.scan(step(down_w, down_b), d0, xs[1:])
        D = jnp.concatenate([d0[None], d_rest], 0)
        seq = jnp.concatenate([D[Hh - 3::-1], D[Hh - 1:Hh]], 0)
        u0 = D[Hh - 1]
        _, u_rest = jax.lax.scan(step(down_w, down_b), u0, seq)
        U = jnp.concatenate([u0[None], u_rest], 0)[::-1]
        ws = jnp.moveaxis(jnp.moveaxis(U, 0, 2), 3, 0)
        r0 = ws[0]
        _, r_rest = jax.lax.scan(step(right_w, right_b), r0, ws[1:])
        R = jnp.concatenate([r0[None], r_rest], 0)
        l0 = R[Ww - 1]
        _, l_rest = jax.lax.scan(step(left_w, left_b), l0, R[Ww - 2::-1])
        L = jnp.concatenate([l0[None], l_rest], 0)[::-1]
        return jnp.moveaxis(L, 0, 3)

    def _L2_conv_ref(x, w_hidden, b_hidden, w_dw, b_dw, gamma, beta, w_out, b_out):
        import jax, jax.numpy as jnp
        import numpy as np
        PATCH = 8
        EPS = 1e-05

        def _conv2d(x, w, b, groups=1, padding='VALID'):
            y = jax.lax.conv_general_dilated(x, w, window_strides=(1, 1), padding=padding, feature_group_count=groups, dimension_numbers=('NCHW', 'OIHW', 'NCHW'))
            return y + b[None, :, None, None]
        B, C, H, W = x.shape
        C6 = 6 * C
        hidden = _conv2d(x, w_hidden, b_hidden)
        qkv = _conv2d(hidden, w_dw, b_dw, groups=C6, padding='SAME')
        q, k, v = jnp.split(qkv, 3, axis=1)
        C2 = 2 * C
        hp, wp = (H // PATCH, W // PATCH)
        q_patch = q.reshape(B, C2, hp, wp, PATCH, PATCH)
        k_patch = k.reshape(B, C2, hp, wp, PATCH, PATCH)
        q_fft = jnp.fft.rfft2(q_patch)
        k_fft = jnp.fft.rfft2(k_patch)
        out = jnp.fft.irfft2(q_fft * k_fft, s=(PATCH, PATCH))
        out = out.reshape(B, C2, H, W)
        mu = jnp.mean(out, axis=1, keepdims=True)
        var = jnp.var(out, axis=1, keepdims=True)
        normed = (out - mu) / jnp.sqrt(var + EPS)
        normed = normed * gamma[None, :, None, None] + beta[None, :, None, None]
        return _conv2d(v * normed, w_out, b_out)

    def _L3_conv_ref(x, w_in, w_dw, fft_mask, w_out):
        import jax, jax.numpy as jnp
        from jax import lax
        import numpy as np
        DIM = 48
        EXPANSION = 3.0
        P = 8
        HIDDEN = int(DIM * EXPANSION)
        C2 = HIDDEN * 2
        B, C, H, W = x.shape
        y = jnp.einsum('oc,bchw->bohw', w_in, x)
        hp = -H % P
        wp = -W % P
        if hp or wp:
            y = jnp.pad(y, ((0, 0), (0, 0), (0, hp), (0, wp)), mode='reflect')
        H2, W2 = (H + hp, W + wp)
        ht, wt = (H2 // P, W2 // P)
        yp = y.reshape(B, C2, ht, P, wt, P).transpose(0, 1, 2, 4, 3, 5)
        f = jnp.fft.rfft2(yp) * fft_mask[None]
        yp = jnp.fft.irfft2(f, s=(P, P))
        y = yp.transpose(0, 1, 2, 4, 3, 5).reshape(B, C2, H2, W2)
        if hp or wp:
            y = y[:, :, :H, :W]
        y = lax.conv_general_dilated(y, w_dw, window_strides=(1, 1), padding=((1, 1), (1, 1)), dimension_numbers=('NCHW', 'OIHW', 'NCHW'), feature_group_count=C2)
        x1, x2 = jnp.split(y, 2, axis=1)
        g = jax.nn.gelu(x1, approximate=False) * x2
        return jnp.einsum('oc,bchw->bohw', w_out, g)

    def _gn(v, G=16, eps=1e-5):
        B_, C_, H_, W_ = v.shape
        g = v.reshape(B_, G, C_ // G, H_, W_)
        m = jnp.mean(g, axis=(2, 3, 4), keepdims=True)
        s = jnp.var(g, axis=(2, 3, 4), keepdims=True)
        return ((g - m) / jnp.sqrt(s + eps)).reshape(v.shape)

    def _ln_c(v, eps=1e-6):
        m = jnp.mean(v, axis=1, keepdims=True)
        s = jnp.var(v, axis=1, keepdims=True)
        return (v - m) / jnp.sqrt(s + eps)

    def _ln_t(v, eps=1e-5):
        m = jnp.mean(v, axis=-1, keepdims=True)
        s = jnp.var(v, axis=-1, keepdims=True)
        return (v - m) / jnp.sqrt(s + eps)

    def _to_tokens(v):
        B_, C_, H_, W_ = v.shape
        return v.reshape(B_, C_, H_ * W_).transpose(0, 2, 1)
    def _from_tokens(t, like):
        B_, C_, H_, W_ = like.shape
        return t.transpose(0, 2, 1).reshape(B_, C_, H_, W_)

    x = x + _L0_conv_ref(_gn(x), L0_conv_qkv_w, L0_conv_dw_w, L0_conv_proj_w, L0_conv_temperature)
    x = x + _L1_conv_ref(_gn(x), L1_conv_down_w, L1_conv_down_b, L1_conv_right_w, L1_conv_right_b, L1_conv_left_w, L1_conv_left_b)
    x = x + _L2_conv_ref(_gn(x), L2_conv_w_hidden, L2_conv_b_hidden, L2_conv_w_dw, L2_conv_b_dw, L2_conv_gamma, L2_conv_beta, L2_conv_w_out, L2_conv_b_out)
    x = x + _L3_conv_ref(_gn(x), L3_conv_w_in, L3_conv_w_dw, L3_conv_fft_mask, L3_conv_w_out)
    return x


_drawn_inputs = setup_inputs


def setup_inputs(seed=0):
    import zlib

    import numpy as np

    out = dict(_drawn_inputs(seed))
    spreads = {'L2_conv_b_hidden': (0.0, 0.1),
     'L2_conv_b_dw': (0.0, 0.1),
     'L2_conv_gamma': (1.0, 0.2),
     'L2_conv_beta': (0.0, 0.1),
     'L2_conv_b_out': (0.0, 0.1)}
    factors = {}
    for name, (base, spread) in spreads.items():
        noise = np.random.default_rng([zlib.crc32(name.encode()), seed]).standard_normal(out[name].shape)
        drawn = base * np.exp(spread * noise) if base else spread * noise
        out[name] = jnp.asarray(drawn.astype(out[name].dtype))
    for name, factor in factors.items():
        out[name] = (out[name] * factor).astype(out[name].dtype)
    return out
```

```python
from contextlib import ExitStack

import numpy as np
import concourse.bass as bass
from concourse import mybir
from concourse.alu_op_type import AluOpType as ALU

F32 = mybir.dt.float32
ACT = mybir.ActivationFunctionType
AX = mybir.AxisListType

B, C, H, W = 4, 48, 256, 256
PH, PW = H + 2, W + 2
PH3 = 266
GROUP_EPS = 1e-5
K2 = 2 * C + 2
R = 8
NBLK = H // R
HI = 64
PP = HI + C
C2 = 2 * C
C6 = 6 * C
SLOTS = 94


def _pairs():
    real = [(0, 0), (0, 4), (4, 0), (4, 4)]
    pairs = [(ky, kx) for kx in (1, 2, 3) for ky in range(8)] + [(ky, kx) for kx in (0, 4) for ky in (1, 2, 3)]
    return real, pairs


def _angle(ky, kx):
    y, x = np.meshgrid(np.arange(8), np.arange(8), indexing="ij")
    return 2 * np.pi * (ky * y + kx * x) / 8


def shape_constants():
    real, pairs = _pairs()
    c = {}
    ones = np.zeros((2, PH3, PW), np.float32)
    for k in range(2):
        ones[k, 1 - k:H + 1 - k, 1:W + 1] = 1
    c["k_ones"] = ones
    e1 = np.zeros((C + 1, K2), np.float32)
    e2 = np.zeros((C + 1, K2), np.float32)
    for ch in range(C):
        e1[ch, ch] = e1[ch, C + ch] = 1
    e1[C, 2 * C:] = 1
    e2[:C, 2 * C:] = 1
    c["k_e1"], c["k_e2"] = e1, e2
    sel = np.zeros((128, 128), np.float32)
    batch = np.zeros((128, B), np.float32)
    for p in range(128):
        batch[p, p // 32] = 1
        for ch in range(C):
            if (p // 2) % 16 == ch // 3:
                sel[p, ch] = sel[p, HI + ch] = 0.5
    c["k_sel"], c["k_batch"] = sel, batch
    row = np.zeros((128, 2), np.float32)
    row[:, 0] = 1
    row[C, 0], row[C, 1] = 0, 1
    c["k_onesrow"] = row
    c["k_ident"] = np.eye(128, dtype=np.float32)
    a = np.zeros((128, 2, C2), np.float32)
    inv = np.zeros((SLOTS, 64), np.float32)
    for s, (ky, kx) in enumerate(real):
        co = np.cos(_angle(ky, kx)).ravel()
        a[:64, 0, s] = co
        inv[s] = co / 64
    for n, (ky, kx) in enumerate(pairs):
        s = 4 + 3 * n
        co, si = np.cos(_angle(ky, kx)).ravel(), np.sin(_angle(ky, kx)).ravel()
        a[:64, 0, s], a[:64, 0, s + 1], a[:64, 0, s + 2] = co, -si, co - si
        inv[s], inv[s + 1], inv[s + 2] = (co + si) / 32, (si - co) / 32, -si / 32
    a[64:, 1] = a[:64, 0]
    c["k_a"], c["k_c"] = a, inv
    c["k_mean"] = np.full((C2, C2), 1 / C2, np.float32)
    c["k_center"] = (np.eye(C2) - 1 / C2).astype(np.float32)
    f = np.zeros((8, 2, 8, 2, 64), np.float32)
    g = np.zeros((2, 64, 8, 2, 8), np.float32)
    for p in range(2):
        for s, (ky, kx) in enumerate(real):
            co = np.cos(_angle(ky, kx))
            f[:, p, :, p, s] = co
            g[p, s, :, p, :] = co / 64
        for n, (ky, kx) in enumerate(pairs):
            co, si = np.cos(_angle(ky, kx)), np.sin(_angle(ky, kx))
            f[:, p, :, p, 4 + 2 * n], f[:, p, :, p, 5 + 2 * n] = co, si
            g[p, 4 + 2 * n, :, p, :], g[p, 5 + 2 * n, :, p, :] = co / 32, si / 32
    c["k_f"], c["k_g"] = f.reshape(128, 128), g.reshape(128, 128)
    return c


def lay_out(i):
    d = {}
    xp = np.zeros((B, C, PH, PW), np.float32)
    xp[:, :, 1:H + 1, 1:W + 1] = i["x"]
    d["x_in"] = xp

    def with_bias(w, b):
        out = np.zeros((C + 1, w.shape[0]), np.float32)
        out[:C] = w.reshape(w.shape[0], C).T
        if b is not None:
            out[C] = b
        return out

    def by_row(first, second, n):
        out = np.zeros((K2, n), np.float32)
        for rows, w in (((0, C), first), ((C, 2 * C), second)):
            if w is not None:
                out[rows[0]:rows[1]] = w
        if first is not None:
            out[2 * C] = first
        if second is not None:
            out[2 * C + 1] = second
        return out

    def taps(dw):
        n = dw.shape[0]
        out = np.zeros((K2, 6, n), np.float32)
        for dx in range(3):
            out[:, dx] = by_row(dw[:, 0, 0, dx], dw[:, 0, 1, dx], n)
            out[:, 3 + dx] = by_row(None, dw[:, 0, 2, dx], n)
        return out

    qkv, dw = i["L0_conv_qkv_w"], i["L0_conv_dw_w"]
    d["l0_wqk"] = with_bias(qkv[:2 * C], None)
    d["l0_wv"] = np.zeros((C + 1, 2 * C), np.float32)
    d["l0_wv"][:C, :C] = qkv[2 * C:].reshape(C, C).T
    d["l0_dwqk"] = taps(dw[:2 * C])
    dv = dw[2 * C:, 0]
    out = np.zeros((C, 12, K2), np.float32)
    for pair in range(2):
        for dx in range(3):
            for s in range(2):
                for half in range(2):
                    dy = 2 * pair + half - s
                    if 0 <= dy < 3:
                        k = (pair * 3 + dx) * 2 + s
                        out[:, k, half * C:(half + 1) * C] = dv[:, dy, dx][:, None]
                        out[:, k, 2 * C + half] = dv[:, dy, dx]
    d["l0_dwv"] = out
    d["l0_proj"] = np.ascontiguousarray(i["L0_conv_proj_w"].reshape(C, C).T)
    d["l0_temp"] = np.repeat(i["L0_conv_temperature"].reshape(1, 1), C, axis=0)

    w1 = np.zeros((C2, 3, 3, C2), np.float32)
    b1 = np.zeros((C2, 3), np.float32)
    for n, name in enumerate(("down", "right", "left")):
        w = i[f"L1_conv_{name}_w"]
        for q in range(2):
            b1[q * C:q * C + C, n] = i[f"L1_conv_{name}_b"]
            for p in range(2):
                for s in range(3):
                    k = 2 * (s - 1) + q - p + 2
                    if 0 <= k < 5:
                        w1[q * C:q * C + C, n, s, p * C:p * C + C] = w[:, :, k].T
    d["l1_w"], d["l1_b"] = w1, b1

    d["l2_w"] = with_bias(i["L2_conv_w_hidden"], i["L2_conv_b_hidden"])
    d["l2_dw"] = taps(i["L2_conv_w_dw"])
    badd = np.zeros((K2, C6), np.float32)
    badd[2 * C + 1] = i["L2_conv_b_dw"]
    d["l2_bdw"] = badd
    d["l2_gb"] = np.stack([i["L2_conv_gamma"], i["L2_conv_beta"]], axis=1)
    d["l2_bout"] = i["L2_conv_b_out"].reshape(C, 1)
    d["l2_wout"] = np.ascontiguousarray(i["L2_conv_w_out"].reshape(C, C2).T)

    chans = np.array([half * 3 * C + j * C + ch for j in range(3) for half in range(2) for ch in range(C)])
    d["l3_win"] = np.ascontiguousarray(i["L3_conv_w_in"][chans].T)
    real, pairs = _pairs()
    fm = i["L3_conv_fft_mask"].reshape(C6, 8, 5)[chans]
    ma = np.zeros((2, 64, C6), np.float32)
    mb = np.zeros((2, 64, C6), np.float32)
    for s, (ky, kx) in enumerate(real):
        ma[:, s] = mb[:, s] = fm[:, ky, kx]
    for n, (ky, kx) in enumerate(pairs):
        other = (8 - ky) % 8 if kx in (0, 4) else ky
        ma[:, 4 + 2 * n] = ma[:, 5 + 2 * n] = fm[:, ky, kx]
        mb[:, 4 + 2 * n] = mb[:, 5 + 2 * n] = fm[:, other, kx]
    d["l3_ma"], d["l3_mb"] = ma.reshape(128, C6), mb.reshape(128, C6)
    dw3 = np.zeros((PP, 3, 9), np.float32)
    for j in range(3):
        for half in range(2):
            at = half * 3 * C + j * C
            dw3[half * HI:half * HI + C, j] = i["L3_conv_w_dw"][at:at + C].reshape(C, 9)
    d["l3_dw"] = dw3
    wout = np.zeros((C, 3, 2 * C), np.float32)
    wout[:, :, :C] = i["L3_conv_w_out"].T.reshape(3, C, C).transpose(1, 0, 2)
    d["l3_wout"] = wout
    return d


def rows2(ap):
    return ap.rearrange("c h w -> c (h w)")


def stage_setup(nc, D, S):
    with ExitStack() as ctx:
        zeros = ctx.enter_context(nc.sbuf_tensor("zeros", [C2, (PH3 - H - 1) * PW], F32))
        loaded = ctx.enter_context(nc.semaphore("setup_loaded"))
        zeroed = ctx.enter_context(nc.semaphore("setup_zeroed"))
        stored = ctx.enter_context(nc.semaphore("setup_stored"))
        block = ctx.enter_context(nc.Block())
        names = ["k_sel", "k_batch", "k_onesrow", "k_ident", "k_e1", "k_e2"]

        @block.sync
        def _(sp):
            for name in names:
                sp.dma_start(S[name][:], D[name]).then_inc(loaded, 16)
            sp.wait_ge(loaded, 16 * len(names))

        @block.vector
        def _(dve):
            nc.vector.memset(zeros[:], 0.0).then_inc(zeroed, 1)

        @block.scalar
        def _(act):
            act.wait_ge(zeroed, 1)
            n = 0
            for name, last in (("x1", PH - H - 1), ("x2", PH - H - 1), ("x3", PH3 - H - 1)):
                flat = D[name].rearrange("b c h w -> (b c) h w")
                for k in range(2):
                    part = flat[k * C2:(k + 1) * C2]
                    act.dma_start(part[:, 0, :], zeros[:, 0:PW]).then_inc(stored, 16)
                    act.dma_start(rows2(part[:, H + 1:H + 1 + last, :]), zeros[:, 0:last * PW]).then_inc(stored, 16)
                    n += 2
            act.wait_ge(stored, 16 * n)


def stage_stats(nc, D, S, src, rows, tag):
    chunk = 3 * PW // 2
    per = {PH: 6, PH3: 7}[rows]
    loads, slots = rows // per, 3
    flat = D[src].rearrange("b c h w -> (b c h w)").rearrange("(p n) -> p n", p=128)
    scale = rows * PW / float(H * W)
    gn = S["gn"]
    with ExitStack() as ctx:
        def sb(name, shape):
            return ctx.enter_context(nc.sbuf_tensor(f"{tag}_{name}", shape, F32))

        def sem(name):
            return ctx.enter_context(nc.semaphore(f"{tag}_{name}"))
        part = sb("part", [128, slots, per * chunk])
        stats = sb("stats", [128, rows * 6])
        mv, mom, m2, mb = sb("mv", [128, 2]), sb("mom", [128, 2]), sb("m2", [128, 1]), sb("mb", [128, B, 2])
        ch, var, root = sb("ch", [128, B, 2]), sb("var", [128, B]), sb("root", [128, B])
        ps = ctx.enter_context(nc.psum_tensor(f"{tag}_ps", [128, 512], F32))
        loaded = [sem(f"loaded{k}") for k in range(slots)]
        used, chain, spread, rooted = sem("used"), sem("chain"), sem("spread"), sem("rooted")
        block = ctx.enter_context(nc.Block())

        @block.sync
        def _(sp):
            def load(i, k):
                sp.wait_ge(used, slots * i + k + 1)
                sp.dma_start(part[:, k, :], flat[:, bass.ds((slots * i + k) * (per * chunk), per * chunk)])\
                  .then_inc(loaded[k], 16)
            with sp.Fori(0, loads // slots) as i:
                for k in range(slots):
                    load(i, k)
            for k in range(loads % slots):
                load(loads // slots, k)

        @block.tensor
        def _(pe):
            pe.wait_ge(chain, 5)
            nc.tensor.matmul(ps[:, 0:2 * B], S["k_sel"][:], mb[:].rearrange("p b t -> p (b t)"),
                             start=True, stop=True).then_inc(spread, 1)

        @block.vector
        def _(dve):
            dve.sem_inc(used, slots)

            def take(i, k):
                dve.wait_ge(loaded[k], 16 * (i + 1))
                for j in range(per):
                    last = nc.vector.bn_stats(stats[:, bass.ds(((slots * i + k) * per + j) * 6, 6)],
                                              part[:, k, j * chunk:(j + 1) * chunk])
                last.then_inc(used, 1)
            with dve.Fori(0, loads // slots) as i:
                for k in range(slots):
                    take(i, k)
            for k in range(loads % slots):
                take(loads // slots, k)
            dve.wait_ge(used, slots + loads)
            nc.vector.bn_aggr(mv[:], stats[:]).then_inc(chain, 1)
            dve.wait_ge(chain, 1)
            nc.vector.tensor_tensor(m2[:], mv[:, 0:1], mv[:, 0:1], ALU.mult).then_inc(chain, 1)
            dve.wait_ge(chain, 2)
            nc.vector.tensor_scalar(mom[:, 0:1], mv[:, 0:1], scale, None, ALU.mult).then_inc(chain, 1)
            nc.vector.tensor_scalar(mom[:, 1:2], mv[:, 1:2], m2[:, 0:1], scale, ALU.add, ALU.mult).then_inc(chain, 1)
            dve.wait_ge(chain, 4)
            for b in range(B):
                last = nc.vector.tensor_scalar(mb[:, b, :], mom[:], S["k_batch"][:, b:b + 1], None, ALU.mult)
            last.then_inc(chain, 1)
            dve.wait_ge(spread, 1)
            nc.vector.tensor_copy(ch[:].rearrange("p b t -> p (b t)"), ps[:, 0:2 * B]).then_inc(chain, 1)
            dve.wait_ge(chain, 6)
            nc.vector.tensor_tensor(var[:], ch[:, :, 0], ch[:, :, 0], ALU.mult).then_inc(chain, 1)
            dve.wait_ge(chain, 7)
            nc.vector.tensor_tensor(var[:], ch[:, :, 1], var[:], ALU.subtract).then_inc(chain, 1)
            dve.wait_ge(chain, 8)
            nc.vector.tensor_scalar(var[:], var[:], GROUP_EPS, None, ALU.add).then_inc(chain, 1)
            dve.wait_ge(rooted, 1)
            nc.vector.reciprocal(gn[:, :, 0], root[:]).then_inc(chain, 1)
            dve.wait_ge(chain, 10)
            nc.vector.scalar_tensor_tensor(out=gn[:, :, 1], in0=ch[:, :, 0], scalar=-1.0, in1=gn[:, :, 0],
                                           op0=ALU.mult, op1=ALU.mult).then_inc(chain, 1)
            nc.vector.tensor_scalar(S["gn1"][:], gn[:, :, 0], S["k_onesrow"][:, 0:1], S["k_onesrow"][:, 1:2],
                                    ALU.mult, ALU.add).then_inc(chain, 1)
            dve.wait_ge(chain, 12)

        @block.scalar
        def _(act):
            act.wait_ge(chain, 9)
            nc.scalar.activation(root[:], var[:], ACT.Sqrt).then_inc(rooted, 1)


def load_block(nc, sp, D, src, b, row, T, k, n, sem):
    sp.dma_start(T[0:C, k, :], rows2(D[src][bass.ds(b, 1), :, bass.ds(row, n), :].rearrange("a c h w -> (a c) h w")))\
      .then_inc(sem, 16)
    sp.dma_start(T[C:2 * C, k, :],
                 rows2(D[src][bass.ds(b, 1), :, bass.ds(row + 1, n), :].rearrange("a c h w -> (a c) h w")))\
      .then_inc(sem, 16)
    sp.dma_start(T[2 * C:K2, k, :], rows2(D["k_ones"][:, bass.ds(row, n), :])).then_inc(sem, 16)


def stage_l0_attention(nc, D, S, NB):
    O = 2 * C
    TILES, GT = 2 * R, 4
    GROUPS = TILES // GT
    NCH = 10
    with ExitStack() as ctx:
        def sb(name, shape):
            return ctx.enter_context(nc.sbuf_tensor(f"l0a_{name}", shape, F32))

        def pb(name):
            return ctx.enter_context(nc.psum_tensor(f"l0a_{name}", [128, 512], F32))

        def sem(name):
            return ctx.enter_context(nc.semaphore(f"l0a_{name}"))
        T = sb("T", [K2, 2, (R + 1) * PW])
        qk = sb("qk", [128, GROUPS, GT * O])
        wqk, dwqk, w = sb("wqk", [C + 1, O]), sb("dwqk", [K2, 6, O]), sb("w", [K2, 6, O])
        tmp, lb = sb("tmp", [C + 1, K2]), sb("lb", [C + 1, K2])
        proj, temp = sb("proj", [C, C]), sb("temp", [C, 1])
        zero = sb("zero", [128, O])
        g, gd, gs = sb("g", [O, O]), sb("gd", [O, O]), sb("gs", [O, O])
        n2, rn = sb("n2", [O, 1]), sb("rn", [O, 1])
        sc, e, at = sb("sc", [C, C]), sb("e", [C, C]), sb("at", [C, O])
        mx, sm, rs = sb("mx", [C, 1]), sb("sm", [C, 1]), sb("rs", [C, 1])
        bank = [pb(f"bank{n}") for n in range(GROUPS)]
        gram, small = pb("gram"), pb("small")
        consts, lb_ready, w_psum, w_ready = sem("consts"), sem("lb_ready"), sem("w_psum"), sem("w_ready")
        loaded = [sem(f"loaded{k}") for k in range(2)]
        conv_done = sem("conv_done")
        evac_done, gram_used, zeroed = sem("evac_done"), sem("gram_used"), sem("zeroed")
        gram_ready, chain, turned, exped, mixed = (sem(n) for n in ("gram_ready", "chain", "turned", "exped", "mixed"))
        block = ctx.enter_context(nc.Block())

        @block.sync
        def _(sp):
            for dst, src in ((wqk, "l0_wqk"), (dwqk, "l0_dwqk"), (proj, "l0_proj"), (temp, "l0_temp")):
                sp.dma_start(dst[:], D[src]).then_inc(consts, 16)
            with sp.Fori(0, NB) as b:
                with sp.Fori(0, NBLK // 2) as i:
                    for k in range(2):
                        sp.wait_ge(conv_done, (b * NBLK + 2 * i + k + 1) * GROUPS)
                        load_block(nc, sp, D, "x_in", b, (2 * i + k) * R, T, k, R + 1, loaded[k])

        @block.tensor
        def _(pe):
            def gram_group(n, wait):
                pe.wait_ge(evac_done, wait)
                for t in range(GT):
                    last = nc.tensor.matmul(gram[0:O, 0:O], qk[:, n, t * O:(t + 1) * O], qk[:, n, t * O:(t + 1) * O],
                                            start=False, stop=False, skip_group_check=True)
                last.then_inc(gram_used, 1)
            pe.wait_ge(zeroed, 2)
            with pe.Fori(0, NB) as b:
                pe.wait_ge(lb_ready, b + 1)
                nc.tensor.matmul(small[0:K2, 0:O], lb[:], wqk[:], start=True, stop=True).then_inc(w_psum, 1)
                nc.tensor.matmul(gram[0:O, 0:O], zero[:], zero[:], start=True, stop=False, skip_group_check=True)
                with pe.Fori(0, NBLK // 2) as i:
                    for k in range(2):
                        if k == 0:
                            pe.wait_ge(w_ready, b + 1)
                        pe.wait_ge(loaded[k], (b * (NBLK // 2) + i + 1) * 48)
                        tile = T[:, k, :].rearrange("p (r w) -> p r w", w=PW)
                        for n in range(GROUPS):
                            g0 = (b * NBLK + 2 * i + k) * GROUPS + n
                            pe.wait_ge(evac_done, g0 + 1)
                            for t in range(GT):
                                r, x0 = (n * GT + t) // 2, 128 * (t % 2)
                                for m in range(6):
                                    last = nc.tensor.matmul(
                                        bank[n][:, t * O:(t + 1) * O],
                                        tile[:, r + m // 3, x0 + m % 3:x0 + m % 3 + 128], w[:, m, :],
                                        start=(m == 0), stop=(m == 5))
                            last.then_inc(conv_done, 1)
                            if n > 0:
                                gram_group(n - 1, g0 + GROUPS)
                        gram_group(GROUPS - 1, g0 + GROUPS + 1)
                nc.tensor.matmul(gram[0:O, 0:O], zero[:], zero[:], start=False, stop=True,
                                 skip_group_check=True).then_inc(gram_ready, 1)
                pe.wait_ge(chain, b * NCH + 5)
                nc.tensor.transpose(small[0:O, 128:128 + O], gs[:], S["k_ident"][0:O, 0:O]).then_inc(turned, 1)
                pe.wait_ge(chain, b * NCH + 10)
                nc.tensor.matmul(small[0:O, 256:256 + C], at[:], proj[:], start=True, stop=True).then_inc(mixed, 1)

        @block.scalar
        def _(act):
            with act.Fori(0, NB) as b:
                with act.Fori(0, NBLK) as i:
                    for n in range(GROUPS):
                        g0 = (b * NBLK + i) * GROUPS + n
                        act.wait_ge(conv_done, 2 * GROUPS + g0 + 1)
                        act.wait_ge(gram_used, g0 + 1)
                        nc.scalar.activation(qk[:, n, :], bank[n][:, 0:GT * O], ACT.Copy).then_inc(evac_done, 1)
                act.wait_ge(chain, b * NCH + 3)
                nc.scalar.activation(n2[:], n2[:], ACT.Sqrt).then_inc(exped, 1)
                act.wait_ge(chain, b * NCH + 8)
                nc.scalar.activation(e[:], sc[:], ACT.Exp, bias=mx[:, 0:1], accum_out=sm[:]).then_inc(exped, 1)

        @block.vector
        def _(dve):
            dve.sem_inc(evac_done, GROUPS)
            dve.sem_inc(gram_used, GROUPS)
            dve.sem_inc(conv_done, 2 * GROUPS)
            nc.vector.memset(zero[:], 0.0).then_inc(zeroed, 1)
            nc.vector.memset(at[:], 0.0).then_inc(zeroed, 1)
            dve.wait_ge(consts, 64)
            dve.wait_ge(zeroed, 2)
            with dve.Fori(0, NB) as b:
                norm_weights(nc, dve, S, b, tmp, lb, lb_ready, chain, b * NCH + 1)
                dve.wait_ge(w_psum, b + 1)
                for m in range(6):
                    last = nc.vector.tensor_tensor(w[:, m, :], small[0:K2, 0:O], dwqk[:, m, :], ALU.mult)
                last.then_inc(w_ready, 1)
                dve.wait_ge(gram_ready, b + 1)
                nc.vector.tensor_copy(g[:], gram[0:O, 0:O]).then_inc(chain, 1)
                dve.wait_ge(chain, b * NCH + 2)
                nc.vector.tensor_tensor_reduce(out=gd[:], in0=g[:], in1=S["k_ident"][0:O, 0:O], scale=1.0,
                                               scalar=0.0, op0=ALU.mult, op1=ALU.add, accum_out=n2[:])\
                  .then_inc(chain, 1)
                dve.wait_ge(chain, b * NCH + 3)
                dve.wait_ge(exped, 2 * b + 1)
                nc.vector.tensor_scalar(rn[:], n2[:], 1e-12, None, ALU.max).then_inc(chain, 1)
                dve.wait_ge(chain, b * NCH + 4)
                nc.vector.reciprocal(rn[:], rn[:]).then_inc(turned, 1)
                dve.wait_ge(turned, 2 * b + 1)
                nc.vector.tensor_scalar(gs[:], g[:], rn[:, 0:1], None, ALU.mult).then_inc(chain, 1)
                dve.wait_ge(turned, 2 * b + 2)
                nc.vector.tensor_scalar(sc[:], small[0:C, 128 + C:128 + 2 * C], rn[0:C, 0:1], temp[:, 0:1],
                                        ALU.mult, ALU.mult).then_inc(chain, 1)
                dve.wait_ge(chain, b * NCH + 6)
                nc.vector.tensor_reduce(rs[:], sc[:], AX.X, ALU.max).then_inc(chain, 1)
                dve.wait_ge(chain, b * NCH + 7)
                nc.vector.tensor_scalar(mx[:], rs[:], -1.0, None, ALU.mult).then_inc(chain, 1)
                dve.wait_ge(exped, 2 * b + 2)
                nc.vector.reciprocal(rs[:], sm[:]).then_inc(chain, 1)
                dve.wait_ge(chain, b * NCH + 9)
                nc.vector.tensor_scalar(at[:, 0:C], e[:], rs[:, 0:1], None, ALU.mult).then_inc(chain, 1)
                dve.wait_ge(mixed, b + 1)
                nc.vector.tensor_copy(S["mt"][:, bass.ds(b * C, C)], small[0:C, 256:256 + C])


def norm_weights(nc, dve, S, b, tmp, lb, lb_ready, chain, after):
    nc.vector.tensor_scalar(tmp[:], S["k_e1"][:], S["gn1"][0:C + 1, bass.ds(b, 1)], None, ALU.mult).then_inc(chain, 1)
    dve.wait_ge(chain, after)
    nc.vector.scalar_tensor_tensor(out=lb[:], in0=S["k_e2"][:], scalar=S["gn"][0:C + 1, bass.ds(b, 1), 1],
                                   in1=tmp[:], op0=ALU.mult, op1=ALU.add).then_inc(lb_ready, 1)


def stage_l0_apply(nc, D, S, NB):
    O = 2 * C
    HALF = R // 4
    with ExitStack() as ctx:
        def sb(name, shape):
            return ctx.enter_context(nc.sbuf_tensor(f"l0b_{name}", shape, F32))

        def pb(name):
            return ctx.enter_context(nc.psum_tensor(f"l0b_{name}", [128, 512], F32))

        def sem(name):
            return ctx.enter_context(nc.semaphore(f"l0b_{name}"))
        T = sb("T", [K2, 2, (R + 1) * PW])
        out = sb("out", [O, 2, R // 2, PW])
        wv, dwv, uw, w = sb("wv", [C + 1, O]), sb("dwv", [C, 12, K2]), sb("uw", [C, 12, K2]), sb("w", [K2, 6, O])
        tmp, lb = sb("tmp", [C + 1, K2]), sb("lb", [C + 1, K2])
        bank = [pb(f"bank{n}") for n in range(4)]
        small = [pb("small0"), pb("small1"), pb("small2")]
        consts, lb_ready, chain, v_psum, u_ready, w_psum, w_ready = (
            sem(n) for n in ("consts", "lb_ready", "chain", "v_psum", "u_ready", "w_psum", "w_ready"))
        loaded = [sem(f"loaded{k}") for k in range(2)]
        stored = [sem(f"stored{k}") for k in range(2)]
        conv_done, added, bordered = sem("conv_done"), sem("added"), sem("bordered")
        block = ctx.enter_context(nc.Block())

        @block.sync
        def _(sp):
            for dst, src in ((wv[:], "l0_wv"), (dwv[:], "l0_dwv")):
                sp.dma_start(dst, D[src]).then_inc(consts, 16)
            with sp.Fori(0, NB) as b:
                with sp.Fori(0, NBLK // 2) as i:
                    for k in range(2):
                        sp.wait_ge(added, (b * NBLK + 2 * i + k + 1) * 2)
                        load_block(nc, sp, D, "x_in", b, (2 * i + k) * R, T, k, R + 1, loaded[k])

        @block.scalar
        def _(act):
            with act.Fori(0, NB) as b:
                with act.Fori(0, NBLK // 2) as i:
                    for k in range(2):
                        blk = b * NBLK + 2 * i + k
                        act.wait_ge(added, 4 + (blk + 1) * 2)
                        for s in range(2):
                            dst = D["x1"].rearrange("b c (h s) w -> b c h s w", s=2)
                            dst = dst[bass.ds(b, 1), :, bass.ds((2 * i + k) * (R // 2) + s, R // 2), 1 - s, :]
                            act.dma_start(dst.rearrange("a c h w -> (a c) h w"), out[s * C:(s + 1) * C, k])\
                                .then_inc(stored[k], 16)
            for k in range(2):
                act.wait_ge(stored[k], 32 + 16 * NB * NBLK)

        @block.tensor
        def _(pe):
            with pe.Fori(0, NB) as b:
                pe.wait_ge(lb_ready, b + 1)
                nc.tensor.matmul(small[0][0:O, 0:K2], wv[:], lb[:], start=True, stop=True).then_inc(v_psum, 1)
                pe.wait_ge(u_ready, b + 1)
                for m in range(12):
                    last = nc.tensor.matmul(small[1 + m // 10][0:K2, (m % 10) * C:(m % 10 + 1) * C],
                                            uw[:, m, :], S["mt"][:, bass.ds(b * C, C)], start=True, stop=True)
                last.then_inc(w_psum, 1)
                with pe.Fori(0, NBLK // 2) as i:
                    for k in range(2):
                        if k == 0:
                            pe.wait_ge(w_ready, b + 1)
                        pe.wait_ge(loaded[k], (b * (NBLK // 2) + i + 1) * 48)
                        tile = T[:, k, :].rearrange("p (r w) -> p r w", w=PW)
                        for n in range(2):
                            pe.wait_ge(added, (b * NBLK + 2 * i + k) * 2 + n + 1)
                            for m in range(6):
                                r = 4 * n + 2 * (m // 3)
                                last = nc.tensor.matmul(bank[2 * k + n][0:O, :], w[:, m, :],
                                                        tile[:, r:r + 3:2, m % 3:m % 3 + W],
                                                        start=(m == 0), stop=(m == 5))
                            last.then_inc(conv_done, 1)

        @block.vector
        def _(dve):
            nc.vector.memset(out[:], 0.0).then_inc(bordered, 1)
            dve.sem_inc(added, 4)
            for k in range(2):
                dve.sem_inc(stored[k], 32)
            dve.wait_ge(bordered, 1)
            dve.wait_ge(consts, 32)
            with dve.Fori(0, NB) as b:
                norm_weights(nc, dve, S, b, tmp, lb, lb_ready, chain, b + 1)
                dve.wait_ge(v_psum, b + 1)
                for m in range(12):
                    last = nc.vector.tensor_tensor(uw[:, m, :], small[0][0:C, 0:K2], dwv[:, m, :], ALU.mult)
                last.then_inc(u_ready, 1)
                dve.wait_ge(w_psum, b + 1)
                nc.vector.tensor_copy(w[:].rearrange("p m (s o) -> p (m s) o", s=2)[:, 0:10],
                                      small[1][0:K2, 0:10 * C].rearrange("p (m o) -> p m o", o=C))
                nc.vector.tensor_copy(w[:].rearrange("p m (s o) -> p (m s) o", s=2)[:, 10:12],
                                      small[2][0:K2, 0:2 * C].rearrange("p (m o) -> p m o", o=C)).then_inc(w_ready, 1)
                with dve.Fori(0, NBLK // 2) as i:
                    for k in range(2):
                        tile = T[:, k, :].rearrange("p (r w) -> p r w", w=PW)
                        for n in range(2):
                            dve.wait_ge(conv_done, (b * NBLK + 2 * i + k) * 2 + n + 1)
                            if n == 0:
                                dve.wait_ge(stored[k], (b * (NBLK // 2) + i + 1) * 32)
                            r = 4 * n + 1
                            nc.vector.tensor_tensor(
                                out[:, k, 2 * n:2 * n + 2, 1:W + 1].rearrange("p r (q u) -> p r u q", q=2),
                                bank[2 * k + n][0:O, :].rearrange("p (r u q) -> p r u q", r=2, q=2),
                                tile[0:O, r:r + 3:2, 1:W + 1].rearrange("p r (u q) -> p r u q", q=2),
                                ALU.add).then_inc(added, 1)


def stage_l1_sweeps(nc, D, S, NB):
    HW2 = W // 2
    CH, NCH = 16, 16
    SWEEP = H - 1
    STEPS = 4 * SWEEP
    L = HW2 // 2
    WARM = 5
    DOWN, UP, RIGHT, LEFT = range(4)
    with ExitStack() as ctx:
        def sb(name, shape):
            return ctx.enter_context(nc.sbuf_tensor(f"l1_{name}", shape, F32))

        def sem(name):
            return ctx.enter_context(nc.semaphore(f"l1_{name}"))
        I = sb("image", [C2, H * HW2])
        V = I[:].rearrange("p (h u) -> p h u", u=HW2)
        Hz = I[:].rearrange("p (v w) -> p v w", w=W)
        ring = sb("ring", [C2, 2, CH, HW2 + 2])
        w, bias = sb("w", [C2, 9, C2]), sb("bias", [C2, 3])
        gn = sb("gn", [C2, B, 2])
        warm = sb("warm", [128, 512])
        last_down = sb("last_down", [C2, HW2])
        res = sb("res", [C2, 2, (CH // 2) * W])
        out = sb("out", [C2, 2, CH // 2, PW])
        warm_ps = ctx.enter_context(nc.psum_tensor("l1_warm_ps", [128, 512], F32))
        ps = [ctx.enter_context(nc.psum_tensor(f"l1_ps{k}", [128, 512], F32)) for k in range(2)]
        consts, ready = sem("consts"), sem("ready")
        image_loaded, image_used = [sem("image_loaded0"), sem("image_loaded1")], sem("image_used")
        product = [sem("product0"), sem("product1")]
        state = [sem("state0"), sem("state1")]
        filled, written, kept = sem("filled"), sem("written"), sem("kept")
        copying = sem("copying")
        u_stored, turned, finished, storing = sem("u_stored"), sem("turned"), sem("finished"), sem("storing")
        res_loaded = [sem("res_loaded0"), sem("res_loaded1")]
        stored = [sem("stored0"), sem("stored1")]
        block = ctx.enter_context(nc.Block())

        def steps_done(b, sweep, c):
            return b * STEPS + (c * CH + (1 + sweep * SWEEP + CH - 1))

        def wait_steps(eng, b, sweep, c, more=0):
            for half in range(2):
                eng.wait_ge(state[half], steps_done(b, sweep, c) + more)

        def de_interleaved(dram, b, row, n):
            return dram[bass.ds(b, 1), :, bass.ds(row, n), :].rearrange("a c h w -> (a c) h w")

        def by_parity(dram, b, pair, n, member):
            v = dram.rearrange("b c (v s) w -> b c v s w", s=2)[bass.ds(b, 1), :, bass.ds(pair, n), member, :]
            return v.rearrange("a c v w -> (a c) v w")

        @block.sync
        def _(sp):
            sp.dma_start(w[:].rearrange("p n m -> p (n m)"), D["l1_w"].rearrange("p a s m -> p (a s m)"))\
              .then_inc(consts, 16)
            sp.dma_start(bias[:], D["l1_b"]).then_inc(consts, 16)
            for q in range(2):
                sp.dma_start(gn[q * C:(q + 1) * C], S["gn"][0:C]).then_inc(consts, 16)
            sp.wait_ge(ready, 5)
            with sp.Fori(0, NB) as b:
                with sp.Fori(0, NCH // 2) as j:
                    for k in range(2):
                        c = 2 * j + k
                        sp.wait_ge(finished, b * NCH + c + 1)
                        sp.wait_ge(image_used, b * NCH + c + 1)
                        for q in range(2):
                            src = de_interleaved(D["x1"], b, c * CH + 1, CH)
                            sp.dma_start(V[q * C:q * C + C, bass.ds(c * CH, CH), :],
                                         src[:, :, 1 + q * HW2:1 + (q + 1) * HW2]).then_inc(image_loaded[k], 16)
                with sp.Fori(0, NCH // 2) as j:
                    for k in range(2):
                        c = 2 * j + k
                        m = c * (-1) + (NCH - 1)
                        sp.wait_ge(kept, b + 1)
                        wait_steps(sp, b, UP, c)
                        sp.sem_inc(storing, 1)
                        for q in range(2):
                            sp.dma_start(de_interleaved(D["u"], b, m * CH, CH)[:, :, q * HW2:(q + 1) * HW2],
                                         ring[q * C:q * C + C, k, :, 1:HW2 + 1]).then_inc(u_stored, 16)
                        sp.wait_ge(u_stored, (b * NCH + c + 1) * 32)
                        sp.sem_inc(storing, 1)
                        for q in range(2):
                            sp.dma_start(Hz[q * C:q * C + C, bass.ds(m * (CH // 2), CH // 2), :],
                                         by_parity(D["u"], b, m * (CH // 2), CH // 2, q)).then_inc(turned, 16)

        @block.scalar
        def _(act):
            act.wait_ge(ready, 5)
            act.wait_ge(consts, 64)
            with act.Fori(0, NB) as b:
                back = 1 + b * (3 * NCH)
                backs = {DOWN: 0, RIGHT: NCH, LEFT: 2 * NCH}

                def inner(k):
                    return ring[:, k, :, 1:HW2 + 1]

                def columns(x):
                    return Hz.rearrange("p v (q u) -> p q u v", q=2)[:, :, bass.ds(x * (CH // 2), CH // 2), :]

                def by_column(k):
                    return inner(k).rearrange("p (u q) v -> p q u v", q=2)

                def fill(sweep, j, k):
                    first = isinstance(j, int) and j == 0
                    c = 2 * j + k
                    if not (first and k == 0):
                        wait_steps(act, b, sweep, c, -CH - (CH - 1))
                    if first and sweep in (UP, RIGHT, LEFT) and k == 0:
                        wait_steps(act, b, sweep - 1, NCH - 1)
                    if sweep == UP:
                        if first:
                            act.wait_ge(written, back + NCH)
                        else:
                            act.wait_ge(u_stored, (b * NCH + c - 1) * 32)
                    elif sweep == RIGHT and first:
                        act.wait_ge(turned, (b + 1) * NCH * 32)
                        act.wait_ge(u_stored, (b + 1) * NCH * 32)
                    elif first:
                        act.wait_ge(written, back + backs[sweep])
                    else:
                        act.wait_ge(written, back + backs[sweep] + c - 1)
                    if sweep == DOWN:
                        act.wait_ge(image_loaded[k], (b * (NCH // 2) + j + 1) * 32)
                        act.sem_inc(copying, 1)
                        nc.scalar.activation(inner(k), V[:, bass.ds(c * CH, CH), :], ACT.Identity,
                                             scale=gn[:, bass.ds(b, 1), 0],
                                             bias=gn[:, bass.ds(b, 1), 1]).then_inc(filled, 1)
                        act.sem_inc(image_used, 1)
                    else:
                        act.sem_inc(copying, 1)
                    if sweep == UP:
                        top = c * (-CH) + (H - CH - 1)
                        if first and k == 0:
                            nc.scalar.activation(last_down[:], V[:, H - 1, :], ACT.Copy).then_inc(kept, 1)
                            nc.scalar.activation(inner(k)[:, 0:CH - 1, :], V[:, H - CH - 1:H - 2, :], ACT.Copy)\
                                .then_inc(filled, 1)
                            nc.scalar.activation(inner(k)[:, CH - 1, :], V[:, H - 1, :], ACT.Copy).then_inc(filled, 1)
                        elif isinstance(j, int) and j == NCH // 2 - 1 and k == 1:
                            act.wait_ge(kept, b + 1)
                            nc.scalar.activation(inner(k)[:, 1:CH, :], V[:, 0:CH - 1, :], ACT.Copy).then_inc(filled, 1)
                            nc.scalar.activation(inner(k)[:, 0, :], last_down[:], ACT.Copy).then_inc(filled, 1)
                        else:
                            nc.scalar.activation(inner(k), V[:, bass.ds(top, CH), :], ACT.Copy).then_inc(filled, 1)
                    elif sweep > UP:
                        x = c if sweep == RIGHT else c * (-1) + (NCH - 1)
                        nc.scalar.activation(by_column(k), columns(x), ACT.Copy).then_inc(filled, 1)

                def write_back(sweep, j, k):
                    if sweep == UP:
                        return
                    c = 2 * j + k
                    wait_steps(act, b, sweep, c)
                    act.sem_inc(copying, 1)
                    if sweep == DOWN:
                        nc.scalar.activation(V[:, bass.ds(c * CH, CH), :], inner(k), ACT.Copy).then_inc(written, 1)
                    else:
                        x = c if sweep == RIGHT else c * (-1) + (NCH - 1)
                        nc.scalar.activation(columns(x), by_column(k), ACT.Copy).then_inc(written, 1)

                for sweep in range(4):
                    fill(sweep, 0, 0)
                    fill(sweep, 0, 1)
                    write_back(sweep, 0, 0)
                    with act.Fori(1, NCH // 2 - 1) as j:
                        fill(sweep, j, 0)
                        write_back(sweep, j - 1, 1)
                        fill(sweep, j, 1)
                        write_back(sweep, j, 0)
                    last = NCH // 2 - 1
                    fill(sweep, last, 0)
                    write_back(sweep, last - 1, 1)
                    fill(sweep, last, 1)
                    write_back(sweep, last, 0)
                    write_back(sweep, last, 1)

                def residual(m, k):
                    act.wait_ge(finished, NCH - 2 + b * NCH + m + 1)
                    for q in range(2):
                        src = D["x1"].rearrange("b c (v s) w -> b c v s w", s=2)
                        src = src[bass.ds(b, 1), :, bass.ds(m * (CH // 2) + q, CH // 2), 1 - q, 1:W + 1]
                        act.dma_start(res[q * C:q * C + C, k, :].rearrange("p (v w) -> p v w", w=W),
                                      src.rearrange("a c v w -> (a c) v w")).then_inc(res_loaded[k], 16)

                def store(m, k):
                    act.wait_ge(finished, NCH + b * NCH + m + 1)
                    for q in range(2):
                        act.dma_start(by_parity(D["x2"], b, m * (CH // 2) + q, CH // 2, 1 - q),
                                      out[q * C:q * C + C, k]).then_inc(stored[k], 16)
                for k in range(2):
                    residual(k, k)
                with act.Fori(0, NCH // 2 - 1) as j:
                    for k in range(2):
                        store(2 * j + k, k)
                        residual(2 * j + 2 + k, k)
                for k in range(2):
                    store(NCH - 2 + k, k)
            for k in range(2):
                act.wait_ge(stored[k], 32 + NB * NCH * 16)

        def steps(sweep, j, k):
            for pos in range(1 if isinstance(j, int) and j == 0 and k == 0 else 0, CH):
                if sweep in (DOWN, RIGHT):
                    line, before = pos, pos - 1
                else:
                    line, before = CH - 1 - pos, CH - pos
                slot = k if pos else 1 - k
                yield line, slot, before % CH, pos

        def filled_by(b, sweep, j, k):
            extra = (2 if sweep > UP else 0) + (1 if sweep == UP else 0)
            if sweep == UP and isinstance(j, int) and j == NCH // 2 - 1 and k == 1:
                extra += 1
            return b * (4 * NCH + 2) + 2 * j + (sweep * NCH + k + 1 + extra)

        def each_chunk(eng, work, finish=None):
            with eng.Fori(0, NB) as b:
                for sweep in range(4):
                    for k in range(2):
                        work(b, sweep, 0, k)
                    with eng.Fori(1, NCH // 2 - 1) as j:
                        for k in range(2):
                            work(b, sweep, j, k)
                    for k in range(2):
                        work(b, sweep, NCH // 2 - 1, k)
                if finish:
                    finish(eng, b)

        @block.tensor
        def _(pe):
            pe.wait_ge(consts, 64)
            pe.wait_ge(ready, 5)

            def warm_up():
                for _ in range(WARM):
                    nc.tensor.matmul(warm_ps[:], S["k_ident"][:], warm[:], start=True, stop=True)

            def work(b, sweep, j, k):
                kernel = (0, 0, 1, 2)[sweep]
                if isinstance(j, int) and j == 0 and k == 0:
                    pe.wait_ge(filled, filled_by(b, sweep, 0, 0))
                    warm_up()
                for line, slot, before, pos in steps(sweep, j, k):
                    n = b * STEPS + j * (2 * CH) + (1 + sweep * SWEEP + k * CH + pos - 1)

                    def shifted(half, s):
                        return ring[:, slot, before, s + half * L:s + (half + 1) * L]
                    pe.wait_ge(state[0], n)
                    for s in (0, 1):
                        nc.tensor.matmul(ps[0][0:C2, 0:L], w[:, 3 * kernel + s, :], shifted(0, s),
                                         start=(s == 0), stop=False)
                    pe.wait_ge(state[1], n)
                    nc.tensor.matmul(ps[0][0:C2, 0:L], w[:, 3 * kernel + 2, :], shifted(0, 2), start=False, stop=True)\
                        .then_inc(product[0], 1)
                    for s in (2, 1, 0):
                        last = nc.tensor.matmul(ps[1][0:C2, 0:L], w[:, 3 * kernel + s, :], shifted(1, s),
                                                start=(s == 2), stop=(s == 0))
                    last.then_inc(product[1], 1)
            each_chunk(pe, work)

        @block.vector
        def _(dve):
            nc.vector.memset(ring[:], 0.0).then_inc(ready, 1)
            nc.vector.memset(I[:], 0.0).then_inc(ready, 1)
            nc.vector.memset(warm[:], 0.0).then_inc(ready, 1)
            nc.vector.memset(res[:], 0.0).then_inc(ready, 1)
            nc.vector.memset(out[:], 0.0).then_inc(ready, 1)
            dve.wait_ge(ready, 5)
            dve.sem_inc(image_used, 2)
            dve.sem_inc(written, 1)
            for k in range(2):
                dve.sem_inc(state[k], 1)
                dve.sem_inc(stored[k], 32)
            dve.sem_inc(finished, NCH)
            dve.wait_ge(consts, 64)

            def work(b, sweep, j, k):
                kernel = (0, 0, 1, 2)[sweep]
                dve.wait_ge(filled, filled_by(b, sweep, j, k))
                for line, slot, before, pos in steps(sweep, j, k):
                    n = b * STEPS + j * (2 * CH) + (sweep * SWEEP + k * CH + pos)
                    for half in range(2):
                        x = ring[:, k, line, 1 + half * L:1 + (half + 1) * L]
                        dve.wait_ge(product[half], n)
                        nc.vector.scalar_tensor_tensor(out=x, in0=ps[half][0:C2, 0:L], scalar=bias[:, kernel:kernel + 1],
                                                       in1=x, op0=ALU.add, op1=ALU.add).then_inc(state[half], 1)

            def finish(dve, b):
                with dve.Fori(0, NCH // 2) as j:
                    for k in range(2):
                        m = 2 * j + k
                        dve.wait_ge(written, 1 + (b + 1) * (3 * NCH))
                        dve.wait_ge(stored[k], (b * (NCH // 2) + j + 1) * 32)
                        dve.wait_ge(res_loaded[k], (b * (NCH // 2) + j + 1) * 32)
                        nc.vector.tensor_tensor(
                            out[:, k, :, 1:W + 1].rearrange("p v (u q) -> p v q u", q=2),
                            Hz[:, bass.ds(m * (CH // 2), CH // 2), :].rearrange("p v (q u) -> p v q u", q=2),
                            res[:, k, :].rearrange("p (v q u) -> p v q u", q=2, u=HW2),
                            ALU.add).then_inc(finished, 1)
            each_chunk(dve, work, finish)


def stage_l2(nc, D, S, NB):
    QK = 2 * C2
    GROUPS = R // 2
    with ExitStack() as ctx:
        def sb(name, shape):
            return ctx.enter_context(nc.sbuf_tensor(f"l2_{name}", shape, F32))

        def pb(name):
            return ctx.enter_context(nc.psum_tensor(f"l2_{name}", [128, 512], F32))

        def sem(name):
            return ctx.enter_context(nc.semaphore(f"l2_{name}"))
        T = sb("T", [K2, 2, (R + 1) * PW])
        win, dw, w = sb("win", [C + 1, C6]), sb("dw", [K2, 6, C6]), sb("w", [K2, 6, C6])
        bdw = sb("bdw", [K2, C6])
        tmp, lb = sb("tmp", [C + 1, K2]), sb("lb", [C + 1, K2])
        a, cinv = sb("a", [128, 2, C2]), sb("cinv", [SLOTS, 64])
        mean, center = sb("mean", [C2, C2]), sb("center", [C2, C2])
        gb, bout, wout, eps = sb("gb", [C2, 2]), sb("bout", [C, 1]), sb("wout", [C2, C]), sb("eps", [C2, 1])
        qk = sb("qk", [128, 2, 2 * QK])
        ks = sb("ks", [SLOTS, 2, 2 * C2])
        z = sb("z", [SLOTS, 4, 2 * C2])
        mixed, sq, sd, cn, ga, t = (sb(n, [C2, 512]) for n in ("mixed", "sq", "sd", "cn", "ga", "t"))
        rsd = sb("rsd", [C2, 512])
        out = sb("out", [C, 2, R * PW])
        bq = [pb("q0"), pb("q1")]
        bf = [pb("f0"), pb("f1")]
        bv = [pb("v0"), pb("v1")]
        bx, by = pb("x"), pb("y")
        names = ["consts", "chain", "lb_ready", "w_psum", "w_ready", "bordered",
                 "qk_done", "qk_out", "v_done", "f_done", "k_out", "z_done", "inv_done", "inv_out", "cen_done",
                 "sq_out", "var_done", "sd_out", "rsd_out", "cn_out", "ga_out", "t_out", "proj_done", "res_out"]
        s = {n: sem(n) for n in names}
        loaded = [sem(f"loaded{k}") for k in range(2)]
        stored = [sem(f"stored{k}") for k in range(2)]
        block = ctx.enter_context(nc.Block())

        @block.sync
        def _(sp):
            cs = ((win, "l2_w"), (dw, "l2_dw"), (bdw, "l2_bdw"), (a, "k_a"), (cinv, "k_c"), (mean, "k_mean"),
                  (center, "k_center"), (gb, "l2_gb"), (bout, "l2_bout"), (wout, "l2_wout"))
            assert len(cs) == 10
            for dst, src in cs:
                sp.dma_start(dst[:], D[src]).then_inc(s["consts"], 16)
            with sp.Fori(0, NB) as b:
                with sp.Fori(0, NBLK // 2) as i:
                    for k in range(2):
                        sp.wait_ge(s["res_out"], (b * NBLK + 2 * i + k + 1) * GROUPS)
                        load_block(nc, sp, D, "x2", b, (2 * i + k) * R, T, k, R + 1, loaded[k])

        @block.tensor
        def _(pe):
            def convolve_qk(g, tile, n, half):
                pe.wait_ge(s["qk_out"], g * 2 + half + 1)
                for m2 in range(2):
                    r, x0 = 2 * n + half, 128 * m2
                    for m in range(6):
                        last = nc.tensor.matmul(bq[half][:, m2 * QK:(m2 + 1) * QK],
                                                tile[:, r + m // 3, x0 + m % 3:x0 + m % 3 + 128], w[:, m, 0:QK],
                                                start=(m == 0), stop=(m == 5))
                last.then_inc(s["qk_done"], 1)

            def spectrum(g, m2):
                if m2 % 2 == 0:
                    pe.wait_ge(s["qk_out"], 2 + g * 2 + m2 // 2 + 1)
                pe.wait_ge(s["z_done"], g * 4 + m2 + 1)
                for p in range(2):
                    last = nc.tensor.matmul(bf[m2 % 2][0:SLOTS, p * QK:(p + 1) * QK], a[:, p, 0:SLOTS],
                                            qk[:, m2 // 2, (m2 % 2) * QK:(m2 % 2 + 1) * QK], start=True, stop=True)
                last.then_inc(s["f_done"], 1)

            def convolve_v(g, tile, n):
                pe.wait_ge(s["t_out"], g + 1)
                for m in range(6):
                    r = 2 * n + m // 3
                    last = nc.tensor.matmul(bv[n % 2][0:C2, :], w[:, m, QK:C6], tile[:, r:r + 2, m % 3:m % 3 + W],
                                            start=(m == 0), stop=(m == 5))
                last.then_inc(s["v_done"], 1)

            def inverse(g):
                pe.wait_ge(s["z_done"], 2 + g * 4 + 4)
                for m in range(8):
                    last = nc.tensor.matmul(bx[0:C2, m * 64:(m + 1) * 64],
                                            z[:, m // 2, (m % 2) * C2:(m % 2 + 1) * C2], cinv[:], start=True, stop=True)
                last.then_inc(s["inv_done"], 1)

            def centred(g):
                pe.wait_ge(s["inv_out"], g + 1)
                nc.tensor.matmul(by[0:C2, :], center[:], mixed[:], start=True, stop=True).then_inc(s["cen_done"], 1)

            def variance(g):
                pe.wait_ge(s["sq_out"], g + 1)
                nc.tensor.matmul(bx[0:C2, :], mean[:], sq[:], start=True, stop=True).then_inc(s["var_done"], 1)

            def project(g):
                pe.wait_ge(s["t_out"], 2 + g + 1)
                nc.tensor.matmul(by[0:C, :], wout[:], t[:], start=True, stop=True).then_inc(s["proj_done"], 1)

            with pe.Fori(0, NB) as b:
                pe.wait_ge(s["lb_ready"], b + 1)
                nc.tensor.matmul(bf[0][0:K2, 0:C6], lb[:], win[:], start=True, stop=True).then_inc(s["w_psum"], 1)
                with pe.Fori(0, NBLK // 2) as i:
                    for k in range(2):
                        if k == 0:
                            pe.wait_ge(s["w_ready"], b + 1)
                        pe.wait_ge(loaded[k], (b * (NBLK // 2) + i + 1) * 48)
                        tile = T[:, k, :].rearrange("p (r w) -> p r w", w=PW)
                        for n in range(GROUPS):
                            g = (b * NBLK + 2 * i + k) * GROUPS + n
                            convolve_qk(g, tile, n, 0)
                            convolve_qk(g, tile, n, 1)
                            spectrum(g, 0)
                            spectrum(g, 1)
                            convolve_v(g, tile, n)
                            spectrum(g, 2)
                            spectrum(g, 3)
                            pe.wait_ge(s["sd_out"], 1 + g)
                            inverse(g)
                            pe.wait_ge(s["res_out"], 2 * GROUPS + g)
                            centred(g)
                            variance(g)
                            project(g)

        @block.scalar
        def _(act):
            def read_qk(g, half):
                act.wait_ge(s["qk_done"], g * 2 + half + 1)
                if half == 0:
                    act.wait_ge(s["f_done"], 1 + g * 4)
                nc.scalar.activation(qk[:, half, :], bq[half][:, 0:2 * QK], ACT.Copy).then_inc(s["qk_out"], 1)

            def read_k(g, m2):
                act.wait_ge(s["f_done"], 1 + g * 4 + m2 + 1)
                act.wait_ge(s["z_done"], g * 4 + m2 + 1)
                nc.scalar.activation(ks[:, m2 % 2, :].rearrange("p (h o) -> p h o", h=2),
                                     bf[m2 % 2][0:SLOTS, 0:2 * QK].rearrange("p (h o) -> p h o", h=2)[:, :, C2:QK],
                                     ACT.Copy).then_inc(s["k_out"], 1)

            with act.Fori(0, NB) as b:
                with act.Fori(0, NBLK // 2) as i:
                    for k in range(2):
                        for n in range(GROUPS):
                            g = (b * NBLK + 2 * i + k) * GROUPS + n
                            read_qk(g, 0)
                            read_qk(g, 1)
                            for m2 in range(4):
                                read_k(g, m2)
                            act.wait_ge(s["inv_done"], 1 + g + 1)
                            nc.scalar.activation(mixed[:], bx[0:C2, :], ACT.Copy).then_inc(s["inv_out"], 1)
                            act.wait_ge(s["cen_done"], g + 1)
                            nc.scalar.activation(sq[:], by[0:C2, :], ACT.Square).then_inc(s["sq_out"], 1)
                            act.wait_ge(s["var_done"], g + 1)
                            act.wait_ge(s["cn_out"], 1 + g)
                            nc.scalar.activation(sd[:], bx[0:C2, :], ACT.Sqrt, bias=eps[:, 0:1])\
                                .then_inc(s["sd_out"], 1)
                            act.wait_ge(s["cn_out"], 1 + g + 1)
                            nc.scalar.activation(ga[:], cn[:], ACT.Identity, scale=gb[:, 0:1], bias=gb[:, 1:2])\
                                .then_inc(s["ga_out"], 1)
                        act.wait_ge(s["res_out"], 2 * GROUPS + (b * NBLK + 2 * i + k + 1) * GROUPS)
                        dst = D["x3"][bass.ds(b, 1), :, bass.ds((2 * i + k) * R + 1, R), :]
                        act.dma_start(rows2(dst.rearrange("a c h w -> (a c) h w")), out[:, k, :]).then_inc(stored[k], 16)
            for k in range(2):
                act.wait_ge(stored[k], 16 + 16 * NB * (NBLK // 2))

        @block.vector
        def _(dve):
            nc.vector.memset(out[:], 0.0).then_inc(s["bordered"], 1)
            nc.vector.memset(eps[:], GROUP_EPS).then_inc(s["bordered"], 1)
            for n in ("f_done", "cn_out", "inv_done", "ga_out", "proj_done", "sd_out"):
                dve.sem_inc(s[n], 1)
            dve.sem_inc(s["qk_out"], 2)
            dve.sem_inc(s["z_done"], 2)
            dve.sem_inc(s["t_out"], 2)
            dve.sem_inc(s["res_out"], 2 * GROUPS)
            for k in range(2):
                dve.sem_inc(stored[k], 16)
            dve.wait_ge(s["bordered"], 2)
            dve.wait_ge(s["consts"], 160)
            with dve.Fori(0, NB) as b:
                norm_weights(nc, dve, S, b, tmp, lb, s["lb_ready"], s["chain"], 2 * b + 1)
                dve.wait_ge(s["w_psum"], b + 1)
                for m in range(6):
                    last = nc.vector.tensor_tensor(w[:, m, :], bf[0][0:K2, 0:C6], dw[:, m, :], ALU.mult)
                last.then_inc(s["chain"], 1)
                dve.wait_ge(s["chain"], 2 * b + 2)
                nc.vector.tensor_tensor(w[:, 1, :], w[:, 1, :], bdw[:], ALU.add).then_inc(s["w_ready"], 1)
                with dve.Fori(0, NBLK // 2) as i:
                    for k in range(2):
                        tile = T[:, k, :].rearrange("p (r w) -> p r w", w=PW)
                        for n in range(GROUPS):
                            g = (b * NBLK + 2 * i + k) * GROUPS + n
                            dve.wait_ge(s["inv_done"], 1 + g)
                            for m2 in range(4):
                                dve.wait_ge(s["k_out"], g * 4 + m2 + 1)
                                nc.vector.tensor_tensor(
                                    z[:, m2, :].rearrange("p (h o) -> p h o", h=2),
                                    bf[m2 % 2][0:SLOTS, 0:2 * QK].rearrange("p (h o) -> p h o", h=2)[:, :, 0:C2],
                                    ks[:, m2 % 2, :].rearrange("p (h o) -> p h o", h=2), ALU.mult)\
                                    .then_inc(s["z_done"], 1)
                            dve.wait_ge(s["sd_out"], 1 + g + 1)
                            dve.wait_ge(s["ga_out"], 1 + g)
                            nc.vector.reciprocal(rsd[:], sd[:]).then_inc(s["rsd_out"], 1)
                            dve.wait_ge(s["rsd_out"], g + 1)
                            nc.vector.tensor_tensor(cn[:], by[0:C2, :], rsd[:], ALU.mult).then_inc(s["cn_out"], 1)
                            dve.wait_ge(s["ga_out"], 1 + g + 1)
                            dve.wait_ge(s["v_done"], g + 1)
                            dve.wait_ge(s["proj_done"], 1 + g)
                            nc.vector.tensor_tensor(t[:], bv[n % 2][0:C2, :], ga[:], ALU.mult).then_inc(s["t_out"], 1)
                            dve.wait_ge(s["proj_done"], 1 + g + 1)
                            if n == 0:
                                dve.wait_ge(stored[k], (b * (NBLK // 2) + i + 1) * 16)
                            o = out[:, k, :].rearrange("p (r w) -> p r w", w=PW)
                            nc.vector.scalar_tensor_tensor(
                                out=o[:, 2 * n:2 * n + 2, 1:W + 1],
                                in0=by[0:C, :].rearrange("p (r w) -> p r w", r=2), scalar=bout[:, 0:1],
                                in1=tile[0:C, 2 * n + 1:2 * n + 3, 1:W + 1], op0=ALU.add, op1=ALU.add)\
                                .then_inc(s["res_out"], 1)


def stage_l3(nc, D, S, NB):
    NB3 = NBLK + 1
    SL = 3
    GT = 4
    GROUPS = 2 * R // GT
    WIN = R + 2
    PE_TAPS = (0, 1)
    DVE_TAPS = tuple(t for t in range(9) if t not in PE_TAPS)
    NT = len(DVE_TAPS)
    HR = R // 2
    HN = HR * W
    UNITS = 6
    TILES_OF = ((0, 1), (2, 3, 4), (5, 6, 7), (8, 9, 10), (11, 12, 13), (14, 15))
    NP3 = 3
    with ExitStack() as ctx:
        def sb(name, shape):
            return ctx.enter_context(nc.sbuf_tensor(f"l3_{name}", shape, F32))

        def pb(name):
            return ctx.enter_context(nc.psum_tensor(f"l3_{name}", [128, 512], F32))

        def sem(name):
            return ctx.enter_context(nc.semaphore(f"l3_{name}"))
        T = sb("T", [C + 1, SL, (R + 1) * PW])
        xp = sb("xp", [C + 1, 2, GT * 128])
        win, ln, lt = sb("win", [C, C6]), sb("ln", [C + 1, B, C]), sb("lt", [C, B, C + 1])
        ma, mb, f, fi = sb("ma", [128, C6]), sb("mb", [128, C6]), sb("f", [128, 128]), sb("fi", [128, 128])
        dw, wout = sb("dw", [PP, 3, 9]), sb("wout", [C, 3, C2])
        diag = sb("diag", [PP, 3, len(PE_TAPS), PP])
        xt, xf = sb("xt", [128, 2, GT * C]), sb("xf", [C, 2, GT * 128])
        ym = sb("ym", [128, 2, GT, 3, 2 * HI])
        rows = sb("rows", [PP, 3, SL, WIN * PW])
        acc = sb("acc", [PP, 2, HN])
        gl, gate = sb("gl", [PP, HN]), sb("gate", [C, 2, 3, HN])
        out = sb("out", [C, 2, HN])
        bt, by, bi, bo = pb("t"), [pb("y0"), pb("y1")], [pb("i0"), pb("i1")], pb("o")
        bd = ctx.enter_context(nc.psum_tensor("l3_d", [128, 1024], F32))
        names = ["consts", "ready", "prep", "ln_psum", "ln_ready", "xt_done", "xt_out", "xf_done", "xf_out",
                 "y_done", "ym_out", "i_done", "rows_out", "shifted", "d_done", "tap", "gl_out", "gate_out",
                 "o_done", "res_out", "xp_out", "spreading", "gathering"]
        s = {n: sem(n) for n in names}
        loaded = [sem(f"loaded{k}") for k in range(SL)]
        stored = [sem("stored0"), sem("stored1")]
        FREE = {"ym_out": 2, "rows_out": 2, "tap": NT, "res_out": NP3 + 1, "y_done": GT + 1, "i_done": 4,
                "gate_out": 2, "xt_done": 2, "xf_out": 1, "shifted": 1, "o_done": 1}
        block = ctx.enter_context(nc.Block())

        def window(j, k):
            return rows[:, j, k, :].rearrange("p (r w) -> p r w", w=PW)

        def tap_rows(j, k, r, n, t):
            return window(j, k)[:, r + t // 3:r + t // 3 + n, t % 3:t % 3 + W]

        def turns(eng, turn):
            with eng.Fori(0, NB) as b:
                with eng.Fori(0, NB3 // SL) as i:
                    for k in range(SL):
                        turn(b, b * NB3 + SL * i + k, k, b * (NB3 // SL) + i)
            turn(None, NB * NB3, 0, None)

        @block.sync
        def _(sp):
            cs = ((win, "l3_win"), (ma, "l3_ma"), (mb, "l3_mb"), (f, "k_f"), (fi, "k_g"), (dw, "l3_dw"),
                  (wout, "l3_wout"))
            for dst, src in cs:
                sp.dma_start(dst[:], D[src]).then_inc(s["consts"], 16)
            sp.wait_ge(s["ready"], 6)
            with sp.Fori(0, NB) as b:
                with sp.Fori(0, NB3 // SL) as i:
                    for k in range(SL):
                        n, blk = b * NB3 + SL * i + k, SL * i + k
                        sp.wait_ge(s["res_out"], 1 + NP3 * n)
                        src = D["x3"][bass.ds(b, 1), :, bass.ds(blk * R, R + 1), :]
                        sp.dma_start(T[0:C, k, :], rows2(src.rearrange("a c h w -> (a c) h w"))).then_inc(loaded[k], 16)
                        sp.dma_start(T[C:C + 1, k, :], rows2(D["k_ones"][0:1, bass.ds(blk * R, R + 1), :]))\
                          .then_inc(loaded[k], 16)

        @block.gpsimd
        def _(pool):
            def turn(b, n, k, lap):
                for g in range(GROUPS) if lap is not None else ():
                    if g == 0:
                        pool.wait_ge(loaded[k], (lap + 1) * 32)
                    pool.wait_ge(s["xt_done"], n * GROUPS + g + 1)
                    pool.sem_inc(s["gathering"], 1)
                    tile = T[:, k, :].rearrange("p (r w) -> p r w", w=PW)
                    x0 = 1 + g * GT * 16
                    nc.gpsimd.tensor_copy(xp[:, g % 2, :].rearrange("p (t r x) -> p t r x", t=GT, r=R),
                                          tile[:, 1:R + 1, x0:x0 + GT * 16].rearrange("p r (t x) -> p t r x", t=GT))\
                        .then_inc(s["xp_out"], 1)
                for h in range(2):
                    pool.wait_ge(s["res_out"], FREE["res_out"] + NP3 * n + 2 + h)
                    pool.dma_start(D["out"][bass.ds(n, 1), :, h * HN:(h + 1) * HN].rearrange("a c n -> (a c) n"),
                                   out[:, h, :]).then_inc(stored[h], 16)
            pool.wait_ge(s["ready"], 6)
            for h in range(2):
                pool.dma_start(D["out"][0, :, h * HN:(h + 1) * HN], out[:, h, :]).then_inc(stored[h], 16)
            turns(pool, turn)
            for h in range(2):
                pool.wait_ge(stored[h], 16 * (NB * NB3 + 2))

        @block.tensor
        def _(pe):
            def spread(b, n, k, g):
                G = n * GROUPS + g
                pe.wait_ge(s["xf_out"], 1 + G)
                pe.wait_ge(s["xp_out"], G + 1)
                pe.sem_inc(s["spreading"], 1)
                for t in range(GT):
                    last = nc.tensor.matmul(bt[:, t * C:(t + 1) * C], xp[:, g % 2, t * 128:(t + 1) * 128],
                                            ln[:, bass.ds(b, 1), :].rearrange("p a c -> p (a c)"),
                                            start=True, stop=True)
                last.then_inc(s["xt_done"], 1)

            def spectrum(n, g):
                G = n * GROUPS + g
                pe.wait_ge(s["xt_out"], G + 1)
                for t in range(GT):
                    last = nc.tensor.matmul(bt[0:C, t * 128:(t + 1) * 128], xt[:, g % 2, t * C:(t + 1) * C], f[:],
                                            start=True, stop=True)
                last.then_inc(s["xf_done"], 1)

            def channels(n, m):
                if m % GT == 0:
                    pe.wait_ge(s["xf_out"], 1 + n * GROUPS + m // GT + 1)
                pe.wait_ge(s["ym_out"], n * 2 * R + m + 1)
                t = m % GT
                nc.tensor.matmul(by[m % 2][:, 0:C6], xf[:, (m // GT) % 2, t * 128:(t + 1) * 128], win[:],
                                 start=True, stop=True).then_inc(s["y_done"], 1)

            def inverse(n, g):
                pe.wait_ge(s["ym_out"], FREE["ym_out"] + (n * GROUPS + g + 1) * GT)
                for j in range(3):
                    pe.wait_ge(s["rows_out"], (n * GROUPS + g) * 3 + j + 1)
                    for t in range(GT):
                        last = nc.tensor.matmul(bi[(3 * g + j) % 2][0:PP, t * 128:(t + 1) * 128],
                                                ym[:, g % 2, t, j, 0:PP], fi[:], start=True, stop=True)
                    last.then_inc(s["i_done"], 1)

            def depthwise(n, k, u):
                h, j = u // 3, u % 3
                if u == 0:
                    pe.wait_ge(s["rows_out"], FREE["rows_out"] + n * GROUPS * 3)
                    pe.wait_ge(s["shifted"], 1 + n)
                    pe.wait_ge(s["res_out"], FREE["res_out"] + n * NP3)
                pe.wait_ge(s["tap"], 1 + (n * UNITS + u) * NT)
                for q in range(2):
                    for ti, t in enumerate(PE_TAPS):
                        last = nc.tensor.matmul(bd[0:PP, q * 512:(q + 1) * 512], diag[:, j, ti, :],
                                                tap_rows(j, (k - 1) % SL, h * HR + 2 * q, 2, t),
                                                start=(ti == 0), stop=(ti == len(PE_TAPS) - 1))
                last.then_inc(s["d_done"], 1)

            def project(n, h, q, bank):
                pe.wait_ge(s["gate_out"], FREE["gate_out"] + n * UNITS + 3 * h + 3)
                for j in range(3):
                    last = nc.tensor.matmul(bank, wout[:, j, :], gate[:, h, j, q * 512:(q + 1) * 512],
                                            start=(j == 0), stop=(j == 2))
                return last

            def turn(b, n, k, lap):
                if lap is not None:
                    spread(b, n, k, 0)
                for u in range(UNITS):
                    depthwise(n, k, u)
                    for m in TILES_OF[u] if lap is not None else ():
                        g = m // GT
                        if m % GT == 0:
                            spectrum(n, g)
                        channels(n, m)
                        if m % GT == 1 and g > 0:
                            inverse(n, g - 1)
                        if m % GT == 2 and g < GROUPS - 1:
                            spread(b, n, k, g + 1)
                    if u == 3:
                        pe.wait_ge(s["res_out"], FREE["res_out"] + n * NP3)
                        project(n, 0, 0, bo[0:C2, :]).then_inc(s["o_done"], 1)
                    if u == 4:
                        pe.wait_ge(s["res_out"], FREE["res_out"] + n * NP3 + 1)
                        project(n, 0, 1, bo[0:C2, :]).then_inc(s["o_done"], 1)
                if lap is not None:
                    inverse(n, GROUPS - 1)
                pe.wait_ge(s["tap"], FREE["tap"] + (n * UNITS + UNITS - 1) * NT + 1)
                project(n, 1, 0, bd[0:C2, 0:512])
                project(n, 1, 1, bd[0:C2, 512:1024]).then_inc(s["o_done"], 1)

            pe.wait_ge(s["prep"], 1)
            for b in range(NB):
                last = nc.tensor.matmul(bt[0:C + 1, b * C:(b + 1) * C], lt[:, b, :], S["k_ident"][0:C, 0:C],
                                        start=True, stop=True)
            last.then_inc(s["ln_psum"], 1)
            pe.wait_ge(s["ln_ready"], 1)
            pe.wait_ge(s["consts"], 112)
            turns(pe, turn)

        @block.scalar
        def _(act):
            def turn(b, n, k, lap):
                if lap is not None:
                    act.wait_ge(s["rows_out"], FREE["rows_out"] + n * GROUPS * 3)
                    nc.scalar.activation(rows[:, :, k, 0:2 * PW], rows[:, :, (k - 1) % SL, R * PW:WIN * PW], ACT.Copy)\
                        .then_inc(s["shifted"], 1)

                def read_pixels(g):
                    act.wait_ge(s["xt_done"], FREE["xt_done"] + n * GROUPS + g + 1)
                    nc.scalar.activation(xt[:, g % 2, :], bt[:, 0:GT * C], ACT.Copy).then_inc(s["xt_out"], 1)

                def read_rows(g):
                    for j in range(3):
                        act.wait_ge(s["i_done"], FREE["i_done"] + (n * GROUPS + g) * 3 + j + 1)
                        x0 = 1 + g * GT * 16
                        nc.scalar.activation(
                            window(j, k)[:, 2:WIN, x0:x0 + GT * 16].rearrange("p r (t x) -> p t r x", t=GT),
                            bi[(3 * g + j) % 2][0:PP, :].rearrange("p (t r x) -> p t r x", t=GT, r=R),
                            ACT.Copy).then_inc(s["rows_out"], 1)
                if lap is not None:
                    read_pixels(0)
                for u in range(UNITS):
                    for m in TILES_OF[u] if lap is not None else ():
                        g = m // GT
                        if m % GT == 0:
                            act.wait_ge(s["xf_done"], n * GROUPS + g + 1)
                            act.wait_ge(s["y_done"], 1 + (n * GROUPS + g) * GT)
                            nc.scalar.activation(xf[:, g % 2, :], bt[0:C, :], ACT.Copy).then_inc(s["xf_out"], 1)
                        if m % GT == 1 and g > 0:
                            read_rows(g - 1)
                        if m % GT == 2 and g < GROUPS - 1:
                            read_pixels(g + 1)
                    if u == UNITS - 1 and lap is not None:
                        read_rows(GROUPS - 1)
                    U = n * UNITS + u
                    act.wait_ge(s["tap"], FREE["tap"] + (U + 1) * NT)
                    act.wait_ge(s["gate_out"], FREE["gate_out"] + U)
                    nc.scalar.activation(gl[HI:HI + C, :], acc[0:C, u % 2, :], ACT.Gelu).then_inc(s["gl_out"], 1)
            act.wait_ge(s["ready"], 6)
            turns(act, turn)

        @block.vector
        def _(dve):
            nc.vector.memset(rows[:], 0.0).then_inc(s["ready"], 1)
            nc.vector.memset(ym[:], 0.0).then_inc(s["ready"], 1)
            nc.vector.memset(T[:], 0.0).then_inc(s["ready"], 1)
            nc.vector.memset(acc[:], 0.0).then_inc(s["ready"], 1)
            nc.vector.memset(gl[:], 0.0).then_inc(s["ready"], 1)
            nc.vector.memset(out[:], 0.0).then_inc(s["ready"], 1)
            dve.wait_ge(s["ready"], 6)
            for name, n in FREE.items():
                dve.sem_inc(s[name], n)
            dve.wait_ge(s["consts"], 112)
            for b in range(NB):
                nc.vector.tensor_scalar(lt[:, b, 0:C], S["k_ident"][0:C, 0:C], S["gn"][0:C, b, 0:1], None, ALU.mult)
                last = nc.vector.tensor_copy(lt[:, b, C:C + 1], S["gn"][0:C, b, 1:2])
            last.then_inc(s["prep"], 1)
            for j in range(3):
                for ti, t in enumerate(PE_TAPS):
                    nc.vector.tensor_scalar(diag[:, j, ti, :], S["k_ident"][0:PP, 0:PP], dw[:, j, t:t + 1], None,
                                            ALU.mult)
            nc.vector.tensor_tensor(ma[:], ma[:], mb[:], ALU.add).then_inc(s["prep"], 1)
            dve.wait_ge(s["prep"], 2)
            nc.vector.tensor_scalar(ma[:], ma[:], 0.5, None, ALU.mult).then_inc(s["prep"], 1)
            dve.wait_ge(s["ln_psum"], 1)
            nc.vector.tensor_copy(ln[:, 0:NB, :].rearrange("p b c -> p (b c)"), bt[0:C + 1, 0:NB * C])\
                .then_inc(s["ln_ready"], 1)
            dve.wait_ge(s["prep"], 3)

            def turn(b, n, k, lap):
                def mask(m):
                    g, t = m // GT, m % GT
                    dve.wait_ge(s["y_done"], FREE["y_done"] + n * 2 * R + m + 1)
                    if t == 0:
                        dve.wait_ge(s["i_done"], 1 + (n * GROUPS + g) * 3)
                    nc.vector.tensor_tensor(
                        ym[:, g % 2, t].rearrange("p j (h c) -> p j h c", h=2)[:, :, :, 0:C],
                        by[m % 2][:, 0:C6].rearrange("p (j h c) -> p j h c", j=3, h=2),
                        ma[:].rearrange("p (j h c) -> p j h c", j=3, h=2), ALU.mult).then_inc(s["ym_out"], 1)

                def make_gate(u):
                    U, h, j = n * UNITS + u, u // 3, u % 3
                    dve.wait_ge(s["gl_out"], U + 1)
                    if j == 0:
                        dve.wait_ge(s["o_done"], 1 + n * NP3)
                    nc.vector.tensor_tensor(gate[:, h, j, :], gl[HI:HI + C, :], acc[HI:HI + C, u % 2, :], ALU.mult)\
                        .then_inc(s["gate_out"], 1)

                def residual(h, q, bank, nrow):
                    if q == 0:
                        dve.wait_ge(stored[h], 16 * (n + 1))
                    r = h * HR + 2 * q
                    tile = T[0:C, (k - 1) % SL, :].rearrange("p (r w) -> p r w", w=PW)
                    nc.vector.tensor_tensor(
                        out[:, h, q * 512:q * 512 + nrow * W].rearrange("p (r w) -> p r w", w=W),
                        bank.rearrange("p (r w) -> p r w", w=W), tile[:, r:r + nrow, 1:W + 1], ALU.add)\
                        .then_inc(s["res_out"], 1)

                for u in range(UNITS):
                    U, h, j = n * UNITS + u, u // 3, u % 3
                    todo = list(TILES_OF[u]) if lap is not None else []
                    a = acc[:, u % 2, :].rearrange("p (r w) -> p r w", w=W)
                    for o, t in enumerate(DVE_TAPS):
                        if o == 0:
                            dve.wait_ge(s["d_done"], U + 1)
                            dve.wait_ge(s["gate_out"], 1 + U)
                        else:
                            dve.wait_ge(s["tap"], FREE["tap"] + U * NT + o)
                        nc.vector.scalar_tensor_tensor(
                            out=a, in0=tap_rows(j, (k - 1) % SL, h * HR, HR, t), scalar=dw[:, j, t:t + 1],
                            in1=a if o else bd[0:PP, :].rearrange("p (r w) -> p r w", w=W),
                            op0=ALU.mult, op1=ALU.add).then_inc(s["tap"], 1)
                        if o in (0, 2, 4) and todo:
                            mask(todo.pop(0))
                        if o == 3 and u > 0:
                            make_gate(u - 1)
                        if o == 1 and u == 4:
                            dve.wait_ge(s["o_done"], 1 + n * NP3 + 1)
                            residual(0, 0, bo[0:C, :], 2)
                        if o == 1 and u == 5:
                            dve.wait_ge(s["o_done"], 1 + n * NP3 + 2)
                            residual(0, 1, bo[0:C, :], 2)
                    assert not todo
                make_gate(UNITS - 1)
                dve.wait_ge(s["o_done"], 1 + n * NP3 + 3)
                residual(1, 0, bd[0:C, :], 4)
            turns(dve, turn)


OUTS = {"out": (B * (NBLK + 1) + 1, C, R * W)}
SCRATCH = {"x1": (B, C, PH, PW), "x2": (B, C, PH, PW), "x3": (B, C, PH3, PW), "u": (B, C, H, W)}


def build_program(nc, D, NB=B, stages="0A B1 2 3"):
    with ExitStack() as ctx:
        S = {n: ctx.enter_context(nc.sbuf_tensor(n, shape, F32)) for n, shape in (
            ("k_sel", [128, 128]), ("k_batch", [128, B]), ("k_onesrow", [128, 2]), ("k_ident", [128, 128]),
            ("k_e1", [C + 1, K2]), ("k_e2", [C + 1, K2]), ("gn", [128, B, 2]), ("gn1", [128, B]),
            ("mt", [C, B * C]))}
        stage_setup(nc, D, S)
        if "0" in stages:
            stage_stats(nc, D, S, "x_in", PH, "s0")
        if "A" in stages:
            stage_l0_attention(nc, D, S, NB)
        if "B" in stages:
            stage_l0_apply(nc, D, S, NB)
        if "1" in stages:
            stage_stats(nc, D, S, "x1", PH, "s1")
            stage_l1_sweeps(nc, D, S, NB)
        if "2" in stages:
            stage_stats(nc, D, S, "x2", PH, "s2")
            stage_l2(nc, D, S, NB)
        if "3" in stages:
            stage_stats(nc, D, S, "x3", PH3, "s3")
            stage_l3(nc, D, S, NB)


def by_image(blocks):
    v = blocks[1:].reshape(B, NBLK + 1, C, R, W).transpose(0, 2, 1, 3, 4).reshape(B, C, (NBLK + 1) * R, W)
    return np.ascontiguousarray(v[:, :, 1:H + 1, :])


def kernel(**inputs):
    import concourse.bacc as bacc
    from concourse.bass_utils import run_bass_kernel_spmd

    arrays = {**shape_constants(), **lay_out({n: np.asarray(a) for n, a in inputs.items()})}
    nc = bacc.Bacc("TRN2", target_bir_lowering=False, num_devices=1)
    D = {n: nc.dram_tensor(n + "_dram", a.shape, F32, kind="ExternalInput").ap() for n, a in arrays.items()}
    for n, shape in SCRATCH.items():
        D[n] = nc.dram_tensor(n + "_dram", shape, F32, kind="Internal").ap()
    D["out"] = nc.dram_tensor("out_dram", OUTS["out"], F32, kind="ExternalOutput").ap()
    build_program(nc, D)
    r = run_bass_kernel_spmd(nc, [{n + "_dram": np.ascontiguousarray(a) for n, a in arrays.items()}], core_ids=[0])
    return by_image(r.results[0]["out_dram"])
```

```python
from contextlib import ExitStack

import numpy as np
import concourse.bass as bass
from concourse import mybir
from concourse.alu_op_type import AluOpType as ALU

F32 = mybir.dt.float32
ACT = mybir.ActivationFunctionType
AX = mybir.AxisListType

B, C, H, W = 4, 48, 256, 256
PH, PW = H + 2, W + 2
PH3 = 266
GROUP_EPS = 1e-5
K2 = 2 * C + 2
R = 8
NBLK = H // R
HI = 64
PP = HI + C
C2 = 2 * C
C6 = 6 * C
SLOTS = 94


def _pairs():
    real = [(0, 0), (0, 4), (4, 0), (4, 4)]
    pairs = [(ky, kx) for kx in (1, 2, 3) for ky in range(8)] + [(ky, kx) for kx in (0, 4) for ky in (1, 2, 3)]
    return real, pairs


def _angle(ky, kx):
    y, x = np.meshgrid(np.arange(8), np.arange(8), indexing="ij")
    return 2 * np.pi * (ky * y + kx * x) / 8


def shape_constants():
    real, pairs = _pairs()
    c = {}
    ones = np.zeros((2, PH3, PW), np.float32)
    for k in range(2):
        ones[k, 1 - k:H + 1 - k, 1:W + 1] = 1
    c["k_ones"] = ones
    e1 = np.zeros((C + 1, K2), np.float32)
    e2 = np.zeros((C + 1, K2), np.float32)
    for ch in range(C):
        e1[ch, ch] = e1[ch, C + ch] = 1
    e1[C, 2 * C:] = 1
    e2[:C, 2 * C:] = 1
    c["k_e1"], c["k_e2"] = e1, e2
    sel = np.zeros((128, 128), np.float32)
    batch = np.zeros((128, B), np.float32)
    for p in range(128):
        batch[p, p // 32] = 1
        for ch in range(C):
            if (p // 2) % 16 == ch // 3:
                sel[p, ch] = sel[p, HI + ch] = 0.5
    c["k_sel"], c["k_batch"] = sel, batch
    row = np.zeros((128, 2), np.float32)
    row[:, 0] = 1
    row[C, 0], row[C, 1] = 0, 1
    c["k_onesrow"] = row
    c["k_ident"] = np.eye(128, dtype=np.float32)
    a = np.zeros((128, 2, C2), np.float32)
    inv = np.zeros((SLOTS, 64), np.float32)
    for s, (ky, kx) in enumerate(real):
        co = np.cos(_angle(ky, kx)).ravel()
        a[:64, 0, s] = co
        inv[s] = co / 64
    for n, (ky, kx) in enumerate(pairs):
        s = 4 + 3 * n
        co, si = np.cos(_angle(ky, kx)).ravel(), np.sin(_angle(ky, kx)).ravel()
        a[:64, 0, s], a[:64, 0, s + 1], a[:64, 0, s + 2] = co, -si, co - si
        inv[s], inv[s + 1], inv[s + 2] = (co + si) / 32, (si - co) / 32, -si / 32
    a[64:, 1] = a[:64, 0]
    c["k_a"], c["k_c"] = a, inv
    c["k_mean"] = np.full((C2, C2), 1 / C2, np.float32)
    c["k_center"] = (np.eye(C2) - 1 / C2).astype(np.float32)
    f = np.zeros((8, 2, 8, 2, 64), np.float32)
    g = np.zeros((2, 64, 8, 2, 8), np.float32)
    for p in range(2):
        for s, (ky, kx) in enumerate(real):
            co = np.cos(_angle(ky, kx))
            f[:, p, :, p, s] = co
            g[p, s, :, p, :] = co / 64
        for n, (ky, kx) in enumerate(pairs):
            co, si = np.cos(_angle(ky, kx)), np.sin(_angle(ky, kx))
            f[:, p, :, p, 4 + 2 * n], f[:, p, :, p, 5 + 2 * n] = co, si
            g[p, 4 + 2 * n, :, p, :], g[p, 5 + 2 * n, :, p, :] = co / 32, si / 32
    c["k_f"], c["k_g"] = f.reshape(128, 128), g.reshape(128, 128)
    return c


def lay_out(i):
    d = {}
    xp = np.zeros((B, C, PH, PW), np.float32)
    xp[:, :, 1:H + 1, 1:W + 1] = i["x"]
    d["x_in"] = xp

    def with_bias(w, b):
        out = np.zeros((C + 1, w.shape[0]), np.float32)
        out[:C] = w.reshape(w.shape[0], C).T
        if b is not None:
            out[C] = b
        return out

    def by_row(first, second, n):
        out = np.zeros((K2, n), np.float32)
        for rows, w in (((0, C), first), ((C, 2 * C), second)):
            if w is not None:
                out[rows[0]:rows[1]] = w
        if first is not None:
            out[2 * C] = first
        if second is not None:
            out[2 * C + 1] = second
        return out

    def taps(dw):
        n = dw.shape[0]
        out = np.zeros((K2, 6, n), np.float32)
        for dx in range(3):
            out[:, dx] = by_row(dw[:, 0, 0, dx], dw[:, 0, 1, dx], n)
            out[:, 3 + dx] = by_row(None, dw[:, 0, 2, dx], n)
        return out

    qkv, dw = i["L0_conv_qkv_w"], i["L0_conv_dw_w"]
    d["l0_wqk"] = with_bias(qkv[:2 * C], None)
    d["l0_wv"] = np.zeros((C + 1, 2 * C), np.float32)
    d["l0_wv"][:C, :C] = qkv[2 * C:].reshape(C, C).T
    d["l0_dwqk"] = taps(dw[:2 * C])
    dv = dw[2 * C:, 0]
    out = np.zeros((C, 12, K2), np.float32)
    for pair in range(2):
        for dx in range(3):
            for s in range(2):
                for half in range(2):
                    dy = 2 * pair + half - s
                    if 0 <= dy < 3:
                        k = (pair * 3 + dx) * 2 + s
                        out[:, k, half * C:(half + 1) * C] = dv[:, dy, dx][:, None]
                        out[:, k, 2 * C + half] = dv[:, dy, dx]
    d["l0_dwv"] = out
    d["l0_proj"] = np.ascontiguousarray(i["L0_conv_proj_w"].reshape(C, C).T)
    d["l0_temp"] = np.repeat(i["L0_conv_temperature"].reshape(1, 1), C, axis=0)

    w1 = np.zeros((C2, 3, 3, C2), np.float32)
    b1 = np.zeros((C2, 3), np.float32)
    for n, name in enumerate(("down", "right", "left")):
        w = i[f"L1_conv_{name}_w"]
        for q in range(2):
            b1[q * C:q * C + C, n] = i[f"L1_conv_{name}_b"]
            for p in range(2):
                for s in range(3):
                    k = 2 * (s - 1) + q - p + 2
                    if 0 <= k < 5:
                        w1[q * C:q * C + C, n, s, p * C:p * C + C] = w[:, :, k].T
    d["l1_w"], d["l1_b"] = w1, b1

    d["l2_w"] = with_bias(i["L2_conv_w_hidden"], i["L2_conv_b_hidden"])
    QK = 2 * C2
    d["l2_dw"] = taps(i["L2_conv_w_dw"])
    d["l2_dw"][:, :, QK:] = 0
    for half in range(2):
        d["l2_dw"][half * C:(half + 1) * C, half, QK:] = 1
        d["l2_dw"][2 * C + half, half, QK:] = 1
    badd = np.zeros((K2, C6), np.float32)
    badd[2 * C + 1, :QK] = i["L2_conv_b_dw"][:QK]
    d["l2_bdw"] = badd
    d["l2_dwv"] = np.concatenate([i["L2_conv_w_dw"][QK:].reshape(C2, 9), i["L2_conv_b_dw"][QK:, None]], axis=1)
    d["l2_gb"] = np.stack([i["L2_conv_gamma"], i["L2_conv_beta"]], axis=1)
    d["l2_bout"] = i["L2_conv_b_out"].reshape(C, 1)
    d["l2_wout"] = np.ascontiguousarray(i["L2_conv_w_out"].reshape(C, C2).T)

    chans = np.array([half * 3 * C + j * C + ch for j in range(3) for half in range(2) for ch in range(C)])
    d["l3_win"] = np.ascontiguousarray(i["L3_conv_w_in"][chans].T)
    real, pairs = _pairs()
    fm = i["L3_conv_fft_mask"].reshape(C6, 8, 5)[chans]
    ma = np.zeros((2, 64, C6), np.float32)
    mb = np.zeros((2, 64, C6), np.float32)
    for s, (ky, kx) in enumerate(real):
        ma[:, s] = mb[:, s] = fm[:, ky, kx]
    for n, (ky, kx) in enumerate(pairs):
        other = (8 - ky) % 8 if kx in (0, 4) else ky
        ma[:, 4 + 2 * n] = ma[:, 5 + 2 * n] = fm[:, ky, kx]
        mb[:, 4 + 2 * n] = mb[:, 5 + 2 * n] = fm[:, other, kx]
    d["l3_ma"], d["l3_mb"] = ma.reshape(128, C6), mb.reshape(128, C6)
    dw3 = np.zeros((PP, 3, 9), np.float32)
    for j in range(3):
        for half in range(2):
            at = half * 3 * C + j * C
            dw3[half * HI:half * HI + C, j] = i["L3_conv_w_dw"][at:at + C].reshape(C, 9)
    d["l3_dw"] = dw3
    wout = np.zeros((C, 3, 2 * C), np.float32)
    wout[:, :, :C] = i["L3_conv_w_out"].T.reshape(3, C, C).transpose(1, 0, 2)
    d["l3_wout"] = wout
    return d


def rows2(ap):
    return ap.rearrange("c h w -> c (h w)")


def stage_setup(nc, D, S):
    with ExitStack() as ctx:
        zeros = ctx.enter_context(nc.sbuf_tensor("zeros", [C2, (PH3 - H - 1) * PW], F32))
        loaded = ctx.enter_context(nc.semaphore("setup_loaded"))
        zeroed = ctx.enter_context(nc.semaphore("setup_zeroed"))
        stored = ctx.enter_context(nc.semaphore("setup_stored"))
        block = ctx.enter_context(nc.Block())
        names = ["k_sel", "k_batch", "k_onesrow", "k_ident", "k_e1", "k_e2"]

        @block.sync
        def _(sp):
            for name in names:
                sp.dma_start(S[name][:], D[name]).then_inc(loaded, 16)
            sp.wait_ge(loaded, 16 * len(names))

        @block.vector
        def _(dve):
            nc.vector.memset(zeros[:], 0.0).then_inc(zeroed, 1)

        @block.scalar
        def _(act):
            act.wait_ge(zeroed, 1)
            n = 0
            for name, last in (("x1", PH - H - 1), ("x2", PH - H - 1), ("x3", PH3 - H - 1)):
                flat = D[name].rearrange("b c h w -> (b c) h w")
                for k in range(2):
                    part = flat[k * C2:(k + 1) * C2]
                    act.dma_start(part[:, 0, :], zeros[:, 0:PW]).then_inc(stored, 16)
                    act.dma_start(rows2(part[:, H + 1:H + 1 + last, :]), zeros[:, 0:last * PW]).then_inc(stored, 16)
                    n += 2
            act.wait_ge(stored, 16 * n)


def stage_stats(nc, D, S, src, rows, tag):
    chunk = 3 * PW // 2
    per = {PH: 6, PH3: 7}[rows]
    loads, slots = rows // per, 3
    flat = D[src].rearrange("b c h w -> (b c h w)").rearrange("(p n) -> p n", p=128)
    scale = rows * PW / float(H * W)
    gn = S["gn"]
    with ExitStack() as ctx:
        def sb(name, shape):
            return ctx.enter_context(nc.sbuf_tensor(f"{tag}_{name}", shape, F32))

        def sem(name):
            return ctx.enter_context(nc.semaphore(f"{tag}_{name}"))
        part = sb("part", [128, slots, per * chunk])
        stats = sb("stats", [128, rows * 6])
        mv, mom, m2, mb = sb("mv", [128, 2]), sb("mom", [128, 2]), sb("m2", [128, 1]), sb("mb", [128, B, 2])
        ch, var, root = sb("ch", [128, B, 2]), sb("var", [128, B]), sb("root", [128, B])
        ps = ctx.enter_context(nc.psum_tensor(f"{tag}_ps", [128, 512], F32))
        loaded = [sem(f"loaded{k}") for k in range(slots)]
        used, chain, spread, rooted = sem("used"), sem("chain"), sem("spread"), sem("rooted")
        block = ctx.enter_context(nc.Block())

        @block.sync
        def _(sp):
            def load(i, k):
                sp.wait_ge(used, slots * i + k + 1)
                sp.dma_start(part[:, k, :], flat[:, bass.ds((slots * i + k) * (per * chunk), per * chunk)])\
                  .then_inc(loaded[k], 16)
            with sp.Fori(0, loads // slots) as i:
                for k in range(slots):
                    load(i, k)
            for k in range(loads % slots):
                load(loads // slots, k)

        @block.tensor
        def _(pe):
            pe.wait_ge(chain, 5)
            nc.tensor.matmul(ps[:, 0:2 * B], S["k_sel"][:], mb[:].rearrange("p b t -> p (b t)"),
                             start=True, stop=True).then_inc(spread, 1)

        @block.vector
        def _(dve):
            dve.sem_inc(used, slots)

            def take(i, k):
                dve.wait_ge(loaded[k], 16 * (i + 1))
                for j in range(per):
                    last = nc.vector.bn_stats(stats[:, bass.ds(((slots * i + k) * per + j) * 6, 6)],
                                              part[:, k, j * chunk:(j + 1) * chunk])
                last.then_inc(used, 1)
            with dve.Fori(0, loads // slots) as i:
                for k in range(slots):
                    take(i, k)
            for k in range(loads % slots):
                take(loads // slots, k)
            dve.wait_ge(used, slots + loads)
            nc.vector.bn_aggr(mv[:], stats[:]).then_inc(chain, 1)
            dve.wait_ge(chain, 1)
            nc.vector.tensor_tensor(m2[:], mv[:, 0:1], mv[:, 0:1], ALU.mult).then_inc(chain, 1)
            dve.wait_ge(chain, 2)
            nc.vector.tensor_scalar(mom[:, 0:1], mv[:, 0:1], scale, None, ALU.mult).then_inc(chain, 1)
            nc.vector.tensor_scalar(mom[:, 1:2], mv[:, 1:2], m2[:, 0:1], scale, ALU.add, ALU.mult).then_inc(chain, 1)
            dve.wait_ge(chain, 4)
            for b in range(B):
                last = nc.vector.tensor_scalar(mb[:, b, :], mom[:], S["k_batch"][:, b:b + 1], None, ALU.mult)
            last.then_inc(chain, 1)
            dve.wait_ge(spread, 1)
            nc.vector.tensor_copy(ch[:].rearrange("p b t -> p (b t)"), ps[:, 0:2 * B]).then_inc(chain, 1)
            dve.wait_ge(chain, 6)
            nc.vector.tensor_tensor(var[:], ch[:, :, 0], ch[:, :, 0], ALU.mult).then_inc(chain, 1)
            dve.wait_ge(chain, 7)
            nc.vector.tensor_tensor(var[:], ch[:, :, 1], var[:], ALU.subtract).then_inc(chain, 1)
            dve.wait_ge(chain, 8)
            nc.vector.tensor_scalar(var[:], var[:], GROUP_EPS, None, ALU.add).then_inc(chain, 1)
            dve.wait_ge(rooted, 1)
            nc.vector.reciprocal(gn[:, :, 0], root[:]).then_inc(chain, 1)
            dve.wait_ge(chain, 10)
            nc.vector.scalar_tensor_tensor(out=gn[:, :, 1], in0=ch[:, :, 0], scalar=-1.0, in1=gn[:, :, 0],
                                           op0=ALU.mult, op1=ALU.mult).then_inc(chain, 1)
            nc.vector.tensor_scalar(S["gn1"][:], gn[:, :, 0], S["k_onesrow"][:, 0:1], S["k_onesrow"][:, 1:2],
                                    ALU.mult, ALU.add).then_inc(chain, 1)
            dve.wait_ge(chain, 12)

        @block.scalar
        def _(act):
            act.wait_ge(chain, 9)
            nc.scalar.activation(root[:], var[:], ACT.Sqrt).then_inc(rooted, 1)


def load_block(nc, sp, D, src, b, row, T, k, n, sem):
    sp.dma_start(T[0:C, k, :], rows2(D[src][bass.ds(b, 1), :, bass.ds(row, n), :].rearrange("a c h w -> (a c) h w")))\
      .then_inc(sem, 16)
    sp.dma_start(T[C:2 * C, k, :],
                 rows2(D[src][bass.ds(b, 1), :, bass.ds(row + 1, n), :].rearrange("a c h w -> (a c) h w")))\
      .then_inc(sem, 16)
    sp.dma_start(T[2 * C:K2, k, :], rows2(D["k_ones"][:, bass.ds(row, n), :])).then_inc(sem, 16)


def stage_l0_attention(nc, D, S, NB):
    O = 2 * C
    TILES, GT = 2 * R, 4
    GROUPS = TILES // GT
    NCH = 10
    with ExitStack() as ctx:
        def sb(name, shape):
            return ctx.enter_context(nc.sbuf_tensor(f"l0a_{name}", shape, F32))

        def pb(name):
            return ctx.enter_context(nc.psum_tensor(f"l0a_{name}", [128, 512], F32))

        def sem(name):
            return ctx.enter_context(nc.semaphore(f"l0a_{name}"))
        T = sb("T", [K2, 2, (R + 1) * PW])
        qk = sb("qk", [128, GROUPS, GT * O])
        wqk, dwqk, w = sb("wqk", [C + 1, O]), sb("dwqk", [K2, 6, O]), sb("w", [K2, 6, O])
        tmp, lb = sb("tmp", [C + 1, K2]), sb("lb", [C + 1, K2])
        proj, temp = sb("proj", [C, C]), sb("temp", [C, 1])
        zero = sb("zero", [128, O])
        g, gd, gs = sb("g", [O, O]), sb("gd", [O, O]), sb("gs", [O, O])
        n2, rn = sb("n2", [O, 1]), sb("rn", [O, 1])
        sc, e, at = sb("sc", [C, C]), sb("e", [C, C]), sb("at", [C, O])
        mx, sm, rs = sb("mx", [C, 1]), sb("sm", [C, 1]), sb("rs", [C, 1])
        bank = [pb(f"bank{n}") for n in range(GROUPS)]
        gram, small = pb("gram"), pb("small")
        consts, lb_ready, w_psum, w_ready = sem("consts"), sem("lb_ready"), sem("w_psum"), sem("w_ready")
        loaded = [sem(f"loaded{k}") for k in range(2)]
        conv_done = sem("conv_done")
        evac_done, gram_used, zeroed = sem("evac_done"), sem("gram_used"), sem("zeroed")
        gram_ready, chain, turned, exped, mixed = (sem(n) for n in ("gram_ready", "chain", "turned", "exped", "mixed"))
        block = ctx.enter_context(nc.Block())

        @block.sync
        def _(sp):
            for dst, src in ((wqk, "l0_wqk"), (dwqk, "l0_dwqk"), (proj, "l0_proj"), (temp, "l0_temp")):
                sp.dma_start(dst[:], D[src]).then_inc(consts, 16)
            with sp.Fori(0, NB) as b:
                with sp.Fori(0, NBLK // 2) as i:
                    for k in range(2):
                        sp.wait_ge(conv_done, (b * NBLK + 2 * i + k + 1) * GROUPS)
                        load_block(nc, sp, D, "x_in", b, (2 * i + k) * R, T, k, R + 1, loaded[k])

        @block.tensor
        def _(pe):
            def gram_group(n, wait):
                pe.wait_ge(evac_done, wait)
                for t in range(GT):
                    last = nc.tensor.matmul(gram[0:O, 0:O], qk[:, n, t * O:(t + 1) * O], qk[:, n, t * O:(t + 1) * O],
                                            start=False, stop=False, skip_group_check=True)
                last.then_inc(gram_used, 1)
            pe.wait_ge(zeroed, 2)
            with pe.Fori(0, NB) as b:
                pe.wait_ge(lb_ready, b + 1)
                nc.tensor.matmul(small[0:K2, 0:O], lb[:], wqk[:], start=True, stop=True).then_inc(w_psum, 1)
                nc.tensor.matmul(gram[0:O, 0:O], zero[:], zero[:], start=True, stop=False, skip_group_check=True)
                with pe.Fori(0, NBLK // 2) as i:
                    for k in range(2):
                        if k == 0:
                            pe.wait_ge(w_ready, b + 1)
                        pe.wait_ge(loaded[k], (b * (NBLK // 2) + i + 1) * 48)
                        tile = T[:, k, :].rearrange("p (r w) -> p r w", w=PW)
                        for n in range(GROUPS):
                            g0 = (b * NBLK + 2 * i + k) * GROUPS + n
                            pe.wait_ge(evac_done, g0 + 1)
                            for t in range(GT):
                                r, x0 = (n * GT + t) // 2, 128 * (t % 2)
                                for m in range(6):
                                    last = nc.tensor.matmul(
                                        bank[n][:, t * O:(t + 1) * O],
                                        tile[:, r + m // 3, x0 + m % 3:x0 + m % 3 + 128], w[:, m, :],
                                        start=(m == 0), stop=(m == 5))
                            last.then_inc(conv_done, 1)
                            if n > 0:
                                gram_group(n - 1, g0 + GROUPS)
                        gram_group(GROUPS - 1, g0 + GROUPS + 1)
                nc.tensor.matmul(gram[0:O, 0:O], zero[:], zero[:], start=False, stop=True,
                                 skip_group_check=True).then_inc(gram_ready, 1)
                pe.wait_ge(chain, b * NCH + 5)
                nc.tensor.transpose(small[0:O, 128:128 + O], gs[:], S["k_ident"][0:O, 0:O]).then_inc(turned, 1)
                pe.wait_ge(chain, b * NCH + 10)
                nc.tensor.matmul(small[0:O, 256:256 + C], at[:], proj[:], start=True, stop=True).then_inc(mixed, 1)

        @block.scalar
        def _(act):
            with act.Fori(0, NB) as b:
                with act.Fori(0, NBLK) as i:
                    for n in range(GROUPS):
                        g0 = (b * NBLK + i) * GROUPS + n
                        act.wait_ge(conv_done, 2 * GROUPS + g0 + 1)
                        act.wait_ge(gram_used, g0 + 1)
                        nc.scalar.activation(qk[:, n, :], bank[n][:, 0:GT * O], ACT.Copy).then_inc(evac_done, 1)
                act.wait_ge(chain, b * NCH + 3)
                nc.scalar.activation(n2[:], n2[:], ACT.Sqrt).then_inc(exped, 1)
                act.wait_ge(chain, b * NCH + 8)
                nc.scalar.activation(e[:], sc[:], ACT.Exp, bias=mx[:, 0:1], accum_out=sm[:]).then_inc(exped, 1)

        @block.vector
        def _(dve):
            dve.sem_inc(evac_done, GROUPS)
            dve.sem_inc(gram_used, GROUPS)
            dve.sem_inc(conv_done, 2 * GROUPS)
            nc.vector.memset(zero[:], 0.0).then_inc(zeroed, 1)
            nc.vector.memset(at[:], 0.0).then_inc(zeroed, 1)
            dve.wait_ge(consts, 64)
            dve.wait_ge(zeroed, 2)
            with dve.Fori(0, NB) as b:
                norm_weights(nc, dve, S, b, tmp, lb, lb_ready, chain, b * NCH + 1)
                dve.wait_ge(w_psum, b + 1)
                for m in range(6):
                    last = nc.vector.tensor_tensor(w[:, m, :], small[0:K2, 0:O], dwqk[:, m, :], ALU.mult)
                last.then_inc(w_ready, 1)
                dve.wait_ge(gram_ready, b + 1)
                nc.vector.tensor_copy(g[:], gram[0:O, 0:O]).then_inc(chain, 1)
                dve.wait_ge(chain, b * NCH + 2)
                nc.vector.tensor_tensor_reduce(out=gd[:], in0=g[:], in1=S["k_ident"][0:O, 0:O], scale=1.0,
                                               scalar=0.0, op0=ALU.mult, op1=ALU.add, accum_out=n2[:])\
                  .then_inc(chain, 1)
                dve.wait_ge(chain, b * NCH + 3)
                dve.wait_ge(exped, 2 * b + 1)
                nc.vector.tensor_scalar(rn[:], n2[:], 1e-12, None, ALU.max).then_inc(chain, 1)
                dve.wait_ge(chain, b * NCH + 4)
                nc.vector.reciprocal(rn[:], rn[:]).then_inc(turned, 1)
                dve.wait_ge(turned, 2 * b + 1)
                nc.vector.tensor_scalar(gs[:], g[:], rn[:, 0:1], None, ALU.mult).then_inc(chain, 1)
                dve.wait_ge(turned, 2 * b + 2)
                nc.vector.tensor_scalar(sc[:], small[0:C, 128 + C:128 + 2 * C], rn[0:C, 0:1], temp[:, 0:1],
                                        ALU.mult, ALU.mult).then_inc(chain, 1)
                dve.wait_ge(chain, b * NCH + 6)
                nc.vector.tensor_reduce(rs[:], sc[:], AX.X, ALU.max).then_inc(chain, 1)
                dve.wait_ge(chain, b * NCH + 7)
                nc.vector.tensor_scalar(mx[:], rs[:], -1.0, None, ALU.mult).then_inc(chain, 1)
                dve.wait_ge(exped, 2 * b + 2)
                nc.vector.reciprocal(rs[:], sm[:]).then_inc(chain, 1)
                dve.wait_ge(chain, b * NCH + 9)
                nc.vector.tensor_scalar(at[:, 0:C], e[:], rs[:, 0:1], None, ALU.mult).then_inc(chain, 1)
                dve.wait_ge(mixed, b + 1)
                nc.vector.tensor_copy(S["mt"][:, bass.ds(b * C, C)], small[0:C, 256:256 + C])


def norm_weights(nc, dve, S, b, tmp, lb, lb_ready, chain, after):
    nc.vector.tensor_scalar(tmp[:], S["k_e1"][:], S["gn1"][0:C + 1, bass.ds(b, 1)], None, ALU.mult).then_inc(chain, 1)
    dve.wait_ge(chain, after)
    nc.vector.scalar_tensor_tensor(out=lb[:], in0=S["k_e2"][:], scalar=S["gn"][0:C + 1, bass.ds(b, 1), 1],
                                   in1=tmp[:], op0=ALU.mult, op1=ALU.add).then_inc(lb_ready, 1)


def stage_l0_apply(nc, D, S, NB):
    O = 2 * C
    HALF = R // 4
    with ExitStack() as ctx:
        def sb(name, shape):
            return ctx.enter_context(nc.sbuf_tensor(f"l0b_{name}", shape, F32))

        def pb(name):
            return ctx.enter_context(nc.psum_tensor(f"l0b_{name}", [128, 512], F32))

        def sem(name):
            return ctx.enter_context(nc.semaphore(f"l0b_{name}"))
        T = sb("T", [K2, 2, (R + 1) * PW])
        out = sb("out", [O, 2, R // 2, PW])
        wv, dwv, uw, w = sb("wv", [C + 1, O]), sb("dwv", [C, 12, K2]), sb("uw", [C, 12, K2]), sb("w", [K2, 6, O])
        tmp, lb = sb("tmp", [C + 1, K2]), sb("lb", [C + 1, K2])
        bank = [pb(f"bank{n}") for n in range(4)]
        small = [pb("small0"), pb("small1"), pb("small2")]
        consts, lb_ready, chain, v_psum, u_ready, w_psum, w_ready = (
            sem(n) for n in ("consts", "lb_ready", "chain", "v_psum", "u_ready", "w_psum", "w_ready"))
        loaded = [sem(f"loaded{k}") for k in range(2)]
        stored = [sem(f"stored{k}") for k in range(2)]
        conv_done, added, bordered = sem("conv_done"), sem("added"), sem("bordered")
        block = ctx.enter_context(nc.Block())

        @block.sync
        def _(sp):
            for dst, src in ((wv[:], "l0_wv"), (dwv[:], "l0_dwv")):
                sp.dma_start(dst, D[src]).then_inc(consts, 16)
            with sp.Fori(0, NB) as b:
                with sp.Fori(0, NBLK // 2) as i:
                    for k in range(2):
                        sp.wait_ge(added, (b * NBLK + 2 * i + k + 1) * 2)
                        load_block(nc, sp, D, "x_in", b, (2 * i + k) * R, T, k, R + 1, loaded[k])

        @block.scalar
        def _(act):
            with act.Fori(0, NB) as b:
                with act.Fori(0, NBLK // 2) as i:
                    for k in range(2):
                        blk = b * NBLK + 2 * i + k
                        act.wait_ge(added, 4 + (blk + 1) * 2)
                        for s in range(2):
                            dst = D["x1"].rearrange("b c (h s) w -> b c h s w", s=2)
                            dst = dst[bass.ds(b, 1), :, bass.ds((2 * i + k) * (R // 2) + s, R // 2), 1 - s, :]
                            act.dma_start(dst.rearrange("a c h w -> (a c) h w"), out[s * C:(s + 1) * C, k])\
                                .then_inc(stored[k], 16)
            for k in range(2):
                act.wait_ge(stored[k], 32 + 16 * NB * NBLK)

        @block.tensor
        def _(pe):
            with pe.Fori(0, NB) as b:
                pe.wait_ge(lb_ready, b + 1)
                nc.tensor.matmul(small[0][0:O, 0:K2], wv[:], lb[:], start=True, stop=True).then_inc(v_psum, 1)
                pe.wait_ge(u_ready, b + 1)
                for m in range(12):
                    last = nc.tensor.matmul(small[1 + m // 10][0:K2, (m % 10) * C:(m % 10 + 1) * C],
                                            uw[:, m, :], S["mt"][:, bass.ds(b * C, C)], start=True, stop=True)
                last.then_inc(w_psum, 1)
                with pe.Fori(0, NBLK // 2) as i:
                    for k in range(2):
                        if k == 0:
                            pe.wait_ge(w_ready, b + 1)
                        pe.wait_ge(loaded[k], (b * (NBLK // 2) + i + 1) * 48)
                        tile = T[:, k, :].rearrange("p (r w) -> p r w", w=PW)
                        for n in range(2):
                            pe.wait_ge(added, (b * NBLK + 2 * i + k) * 2 + n + 1)
                            for m in range(6):
                                r = 4 * n + 2 * (m // 3)
                                last = nc.tensor.matmul(bank[2 * k + n][0:O, :], w[:, m, :],
                                                        tile[:, r:r + 3:2, m % 3:m % 3 + W],
                                                        start=(m == 0), stop=(m == 5))
                            last.then_inc(conv_done, 1)

        @block.vector
        def _(dve):
            nc.vector.memset(out[:], 0.0).then_inc(bordered, 1)
            dve.sem_inc(added, 4)
            for k in range(2):
                dve.sem_inc(stored[k], 32)
            dve.wait_ge(bordered, 1)
            dve.wait_ge(consts, 32)
            with dve.Fori(0, NB) as b:
                norm_weights(nc, dve, S, b, tmp, lb, lb_ready, chain, b + 1)
                dve.wait_ge(v_psum, b + 1)
                for m in range(12):
                    last = nc.vector.tensor_tensor(uw[:, m, :], small[0][0:C, 0:K2], dwv[:, m, :], ALU.mult)
                last.then_inc(u_ready, 1)
                dve.wait_ge(w_psum, b + 1)
                nc.vector.tensor_copy(w[:].rearrange("p m (s o) -> p (m s) o", s=2)[:, 0:10],
                                      small[1][0:K2, 0:10 * C].rearrange("p (m o) -> p m o", o=C))
                nc.vector.tensor_copy(w[:].rearrange("p m (s o) -> p (m s) o", s=2)[:, 10:12],
                                      small[2][0:K2, 0:2 * C].rearrange("p (m o) -> p m o", o=C)).then_inc(w_ready, 1)
                with dve.Fori(0, NBLK // 2) as i:
                    for k in range(2):
                        tile = T[:, k, :].rearrange("p (r w) -> p r w", w=PW)
                        for n in range(2):
                            dve.wait_ge(conv_done, (b * NBLK + 2 * i + k) * 2 + n + 1)
                            if n == 0:
                                dve.wait_ge(stored[k], (b * (NBLK // 2) + i + 1) * 32)
                            r = 4 * n + 1
                            nc.vector.tensor_tensor(
                                out[:, k, 2 * n:2 * n + 2, 1:W + 1].rearrange("p r (q u) -> p r u q", q=2),
                                bank[2 * k + n][0:O, :].rearrange("p (r u q) -> p r u q", r=2, q=2),
                                tile[0:O, r:r + 3:2, 1:W + 1].rearrange("p r (u q) -> p r u q", q=2),
                                ALU.add).then_inc(added, 1)


def stage_l1_sweeps(nc, D, S, NB):
    HW2 = W // 2
    CH, NCH = 16, 16
    SWEEP = H - 1
    STEPS = 4 * SWEEP
    L = HW2 // 2
    WARM = 5
    DOWN, UP, RIGHT, LEFT = range(4)
    with ExitStack() as ctx:
        def sb(name, shape):
            return ctx.enter_context(nc.sbuf_tensor(f"l1_{name}", shape, F32))

        def sem(name):
            return ctx.enter_context(nc.semaphore(f"l1_{name}"))
        I = sb("image", [C2, H * HW2])
        V = I[:].rearrange("p (h u) -> p h u", u=HW2)
        Hz = I[:].rearrange("p (v w) -> p v w", w=W)
        ring = sb("ring", [C2, 2, CH, HW2 + 2])
        w, bias = sb("w", [C2, 9, C2]), sb("bias", [C2, 3])
        gn = sb("gn", [C2, B, 2])
        warm = sb("warm", [128, 512])
        last_down = sb("last_down", [C2, HW2])
        res = sb("res", [C2, 2, (CH // 2) * W])
        out = sb("out", [C2, 2, CH // 2, PW])
        warm_ps = ctx.enter_context(nc.psum_tensor("l1_warm_ps", [128, 512], F32))
        ps = [ctx.enter_context(nc.psum_tensor(f"l1_ps{k}", [128, 512], F32)) for k in range(2)]
        consts, ready = sem("consts"), sem("ready")
        image_loaded, image_used = [sem("image_loaded0"), sem("image_loaded1")], sem("image_used")
        product = [sem("product0"), sem("product1")]
        state = [sem("state0"), sem("state1")]
        filled, written, kept = sem("filled"), sem("written"), sem("kept")
        copying = sem("copying")
        u_stored, turned, finished, storing = sem("u_stored"), sem("turned"), sem("finished"), sem("storing")
        res_loaded = [sem("res_loaded0"), sem("res_loaded1")]
        stored = [sem("stored0"), sem("stored1")]
        block = ctx.enter_context(nc.Block())

        def steps_done(b, sweep, c):
            return b * STEPS + (c * CH + (1 + sweep * SWEEP + CH - 1))

        def wait_steps(eng, b, sweep, c, more=0):
            for half in range(2):
                eng.wait_ge(state[half], steps_done(b, sweep, c) + more)

        def de_interleaved(dram, b, row, n):
            return dram[bass.ds(b, 1), :, bass.ds(row, n), :].rearrange("a c h w -> (a c) h w")

        def by_parity(dram, b, pair, n, member):
            v = dram.rearrange("b c (v s) w -> b c v s w", s=2)[bass.ds(b, 1), :, bass.ds(pair, n), member, :]
            return v.rearrange("a c v w -> (a c) v w")

        @block.sync
        def _(sp):
            sp.dma_start(w[:].rearrange("p n m -> p (n m)"), D["l1_w"].rearrange("p a s m -> p (a s m)"))\
              .then_inc(consts, 16)
            sp.dma_start(bias[:], D["l1_b"]).then_inc(consts, 16)
            for q in range(2):
                sp.dma_start(gn[q * C:(q + 1) * C], S["gn"][0:C]).then_inc(consts, 16)
            sp.wait_ge(ready, 5)
            with sp.Fori(0, NB) as b:
                with sp.Fori(0, NCH // 2) as j:
                    for k in range(2):
                        c = 2 * j + k
                        sp.wait_ge(finished, b * NCH + c + 1)
                        sp.wait_ge(image_used, b * NCH + c + 1)
                        for q in range(2):
                            src = de_interleaved(D["x1"], b, c * CH + 1, CH)
                            sp.dma_start(V[q * C:q * C + C, bass.ds(c * CH, CH), :],
                                         src[:, :, 1 + q * HW2:1 + (q + 1) * HW2]).then_inc(image_loaded[k], 16)
                with sp.Fori(0, NCH // 2) as j:
                    for k in range(2):
                        c = 2 * j + k
                        m = c * (-1) + (NCH - 1)
                        sp.wait_ge(kept, b + 1)
                        wait_steps(sp, b, UP, c)
                        sp.sem_inc(storing, 1)
                        for q in range(2):
                            sp.dma_start(de_interleaved(D["u"], b, m * CH, CH)[:, :, q * HW2:(q + 1) * HW2],
                                         ring[q * C:q * C + C, k, :, 1:HW2 + 1]).then_inc(u_stored, 16)
                        sp.wait_ge(u_stored, (b * NCH + c + 1) * 32)
                        sp.sem_inc(storing, 1)
                        for q in range(2):
                            sp.dma_start(Hz[q * C:q * C + C, bass.ds(m * (CH // 2), CH // 2), :],
                                         by_parity(D["u"], b, m * (CH // 2), CH // 2, q)).then_inc(turned, 16)

        @block.scalar
        def _(act):
            act.wait_ge(ready, 5)
            act.wait_ge(consts, 64)
            with act.Fori(0, NB) as b:
                back = 1 + b * (3 * NCH)
                backs = {DOWN: 0, RIGHT: NCH, LEFT: 2 * NCH}

                def inner(k):
                    return ring[:, k, :, 1:HW2 + 1]

                def columns(x):
                    return Hz.rearrange("p v (q u) -> p q u v", q=2)[:, :, bass.ds(x * (CH // 2), CH // 2), :]

                def by_column(k):
                    return inner(k).rearrange("p (u q) v -> p q u v", q=2)

                def fill(sweep, j, k):
                    first = isinstance(j, int) and j == 0
                    c = 2 * j + k
                    if not (first and k == 0):
                        wait_steps(act, b, sweep, c, -CH - (CH - 1))
                    if first and sweep in (UP, RIGHT, LEFT) and k == 0:
                        wait_steps(act, b, sweep - 1, NCH - 1)
                    if sweep == UP:
                        if first:
                            act.wait_ge(written, back + NCH)
                        else:
                            act.wait_ge(u_stored, (b * NCH + c - 1) * 32)
                    elif sweep == RIGHT and first:
                        act.wait_ge(turned, (b + 1) * NCH * 32)
                        act.wait_ge(u_stored, (b + 1) * NCH * 32)
                    elif first:
                        act.wait_ge(written, back + backs[sweep])
                    else:
                        act.wait_ge(written, back + backs[sweep] + c - 1)
                    if sweep == DOWN:
                        act.wait_ge(image_loaded[k], (b * (NCH // 2) + j + 1) * 32)
                        act.sem_inc(copying, 1)
                        nc.scalar.activation(inner(k), V[:, bass.ds(c * CH, CH), :], ACT.Identity,
                                             scale=gn[:, bass.ds(b, 1), 0],
                                             bias=gn[:, bass.ds(b, 1), 1]).then_inc(filled, 1)
                        act.sem_inc(image_used, 1)
                    else:
                        act.sem_inc(copying, 1)
                    if sweep == UP:
                        top = c * (-CH) + (H - CH - 1)
                        if first and k == 0:
                            nc.scalar.activation(last_down[:], V[:, H - 1, :], ACT.Copy).then_inc(kept, 1)
                            nc.scalar.activation(inner(k)[:, 0:CH - 1, :], V[:, H - CH - 1:H - 2, :], ACT.Copy)\
                                .then_inc(filled, 1)
                            nc.scalar.activation(inner(k)[:, CH - 1, :], V[:, H - 1, :], ACT.Copy).then_inc(filled, 1)
                        elif isinstance(j, int) and j == NCH // 2 - 1 and k == 1:
                            act.wait_ge(kept, b + 1)
                            nc.scalar.activation(inner(k)[:, 1:CH, :], V[:, 0:CH - 1, :], ACT.Copy).then_inc(filled, 1)
                            nc.scalar.activation(inner(k)[:, 0, :], last_down[:], ACT.Copy).then_inc(filled, 1)
                        else:
                            nc.scalar.activation(inner(k), V[:, bass.ds(top, CH), :], ACT.Copy).then_inc(filled, 1)
                    elif sweep > UP:
                        x = c if sweep == RIGHT else c * (-1) + (NCH - 1)
                        nc.scalar.activation(by_column(k), columns(x), ACT.Copy).then_inc(filled, 1)

                def write_back(sweep, j, k):
                    if sweep == UP:
                        return
                    c = 2 * j + k
                    wait_steps(act, b, sweep, c)
                    act.sem_inc(copying, 1)
                    if sweep == DOWN:
                        nc.scalar.activation(V[:, bass.ds(c * CH, CH), :], inner(k), ACT.Copy).then_inc(written, 1)
                    else:
                        x = c if sweep == RIGHT else c * (-1) + (NCH - 1)
                        nc.scalar.activation(columns(x), by_column(k), ACT.Copy).then_inc(written, 1)

                for sweep in range(4):
                    fill(sweep, 0, 0)
                    fill(sweep, 0, 1)
                    write_back(sweep, 0, 0)
                    with act.Fori(1, NCH // 2 - 1) as j:
                        fill(sweep, j, 0)
                        write_back(sweep, j - 1, 1)
                        fill(sweep, j, 1)
                        write_back(sweep, j, 0)
                    last = NCH // 2 - 1
                    fill(sweep, last, 0)
                    write_back(sweep, last - 1, 1)
                    fill(sweep, last, 1)
                    write_back(sweep, last, 0)
                    write_back(sweep, last, 1)

                def residual(m, k):
                    act.wait_ge(finished, NCH - 2 + b * NCH + m + 1)
                    for q in range(2):
                        src = D["x1"].rearrange("b c (v s) w -> b c v s w", s=2)
                        src = src[bass.ds(b, 1), :, bass.ds(m * (CH // 2) + q, CH // 2), 1 - q, 1:W + 1]
                        act.dma_start(res[q * C:q * C + C, k, :].rearrange("p (v w) -> p v w", w=W),
                                      src.rearrange("a c v w -> (a c) v w")).then_inc(res_loaded[k], 16)

                def store(m, k):
                    act.wait_ge(finished, NCH + b * NCH + m + 1)
                    for q in range(2):
                        act.dma_start(by_parity(D["x2"], b, m * (CH // 2) + q, CH // 2, 1 - q),
                                      out[q * C:q * C + C, k]).then_inc(stored[k], 16)
                for k in range(2):
                    residual(k, k)
                with act.Fori(0, NCH // 2 - 1) as j:
                    for k in range(2):
                        store(2 * j + k, k)
                        residual(2 * j + 2 + k, k)
                for k in range(2):
                    store(NCH - 2 + k, k)
            for k in range(2):
                act.wait_ge(stored[k], 32 + NB * NCH * 16)

        def steps(sweep, j, k):
            for pos in range(1 if isinstance(j, int) and j == 0 and k == 0 else 0, CH):
                if sweep in (DOWN, RIGHT):
                    line, before = pos, pos - 1
                else:
                    line, before = CH - 1 - pos, CH - pos
                slot = k if pos else 1 - k
                yield line, slot, before % CH, pos

        def filled_by(b, sweep, j, k):
            extra = (2 if sweep > UP else 0) + (1 if sweep == UP else 0)
            if sweep == UP and isinstance(j, int) and j == NCH // 2 - 1 and k == 1:
                extra += 1
            return b * (4 * NCH + 2) + 2 * j + (sweep * NCH + k + 1 + extra)

        def each_chunk(eng, work, finish=None):
            with eng.Fori(0, NB) as b:
                for sweep in range(4):
                    for k in range(2):
                        work(b, sweep, 0, k)
                    with eng.Fori(1, NCH // 2 - 1) as j:
                        for k in range(2):
                            work(b, sweep, j, k)
                    for k in range(2):
                        work(b, sweep, NCH // 2 - 1, k)
                if finish:
                    finish(eng, b)

        @block.tensor
        def _(pe):
            pe.wait_ge(consts, 64)
            pe.wait_ge(ready, 5)

            def warm_up():
                for _ in range(WARM):
                    nc.tensor.matmul(warm_ps[:], S["k_ident"][:], warm[:], start=True, stop=True)

            def work(b, sweep, j, k):
                kernel = (0, 0, 1, 2)[sweep]
                if isinstance(j, int) and j == 0 and k == 0:
                    pe.wait_ge(filled, filled_by(b, sweep, 0, 0))
                    warm_up()
                for line, slot, before, pos in steps(sweep, j, k):
                    n = b * STEPS + j * (2 * CH) + (1 + sweep * SWEEP + k * CH + pos - 1)

                    def shifted(half, s):
                        return ring[:, slot, before, s + half * L:s + (half + 1) * L]
                    pe.wait_ge(state[0], n)
                    for s in (0, 1):
                        nc.tensor.matmul(ps[0][0:C2, 0:L], w[:, 3 * kernel + s, :], shifted(0, s),
                                         start=(s == 0), stop=False)
                    pe.wait_ge(state[1], n)
                    nc.tensor.matmul(ps[0][0:C2, 0:L], w[:, 3 * kernel + 2, :], shifted(0, 2), start=False, stop=True)\
                        .then_inc(product[0], 1)
                    for s in (2, 1, 0):
                        last = nc.tensor.matmul(ps[1][0:C2, 0:L], w[:, 3 * kernel + s, :], shifted(1, s),
                                                start=(s == 2), stop=(s == 0))
                    last.then_inc(product[1], 1)
            each_chunk(pe, work)

        @block.vector
        def _(dve):
            nc.vector.memset(ring[:], 0.0).then_inc(ready, 1)
            nc.vector.memset(I[:], 0.0).then_inc(ready, 1)
            nc.vector.memset(warm[:], 0.0).then_inc(ready, 1)
            nc.vector.memset(res[:], 0.0).then_inc(ready, 1)
            nc.vector.memset(out[:], 0.0).then_inc(ready, 1)
            dve.wait_ge(ready, 5)
            dve.sem_inc(image_used, 2)
            dve.sem_inc(written, 1)
            for k in range(2):
                dve.sem_inc(state[k], 1)
                dve.sem_inc(stored[k], 32)
            dve.sem_inc(finished, NCH)
            dve.wait_ge(consts, 64)

            def work(b, sweep, j, k):
                kernel = (0, 0, 1, 2)[sweep]
                dve.wait_ge(filled, filled_by(b, sweep, j, k))
                for line, slot, before, pos in steps(sweep, j, k):
                    n = b * STEPS + j * (2 * CH) + (sweep * SWEEP + k * CH + pos)
                    for half in range(2):
                        x = ring[:, k, line, 1 + half * L:1 + (half + 1) * L]
                        dve.wait_ge(product[half], n)
                        nc.vector.scalar_tensor_tensor(out=x, in0=ps[half][0:C2, 0:L], scalar=bias[:, kernel:kernel + 1],
                                                       in1=x, op0=ALU.add, op1=ALU.add).then_inc(state[half], 1)

            def finish(dve, b):
                with dve.Fori(0, NCH // 2) as j:
                    for k in range(2):
                        m = 2 * j + k
                        dve.wait_ge(written, 1 + (b + 1) * (3 * NCH))
                        dve.wait_ge(stored[k], (b * (NCH // 2) + j + 1) * 32)
                        dve.wait_ge(res_loaded[k], (b * (NCH // 2) + j + 1) * 32)
                        nc.vector.tensor_tensor(
                            out[:, k, :, 1:W + 1].rearrange("p v (u q) -> p v q u", q=2),
                            Hz[:, bass.ds(m * (CH // 2), CH // 2), :].rearrange("p v (q u) -> p v q u", q=2),
                            res[:, k, :].rearrange("p (v q u) -> p v q u", q=2, u=HW2),
                            ALU.add).then_inc(finished, 1)
            each_chunk(dve, work, finish)


def stage_l2(nc, D, S, NB):
    QK = 2 * C2
    GROUPS = R // 2
    with ExitStack() as ctx:
        def sb(name, shape):
            return ctx.enter_context(nc.sbuf_tensor(f"l2_{name}", shape, F32))

        def pb(name):
            return ctx.enter_context(nc.psum_tensor(f"l2_{name}", [128, 512], F32))

        def sem(name):
            return ctx.enter_context(nc.semaphore(f"l2_{name}"))
        T = sb("T", [K2, 2, (R + 1) * PW])
        win, dw, w = sb("win", [C + 1, C6]), sb("dw", [K2, 6, C6]), sb("w", [K2, 6, C6])
        bdw = sb("bdw", [K2, C6])
        tmp, lb = sb("tmp", [C + 1, K2]), sb("lb", [C + 1, K2])
        a, cinv = sb("a", [128, 2, C2]), sb("cinv", [SLOTS, 64])
        mean, center = sb("mean", [C2, C2]), sb("center", [C2, C2])
        gb, bout, wout, eps = sb("gb", [C2, 2]), sb("bout", [C, 1]), sb("wout", [C2, C]), sb("eps", [C2, 1])
        qk = sb("qk", [128, 2, 2 * QK])
        ks = sb("ks", [SLOTS, 2, 2 * C2])
        z = sb("z", [SLOTS, 4, 2 * C2])
        mixed, sq, sd, cn, ga, t = (sb(n, [C2, 512]) for n in ("mixed", "sq", "sd", "cn", "ga", "t"))
        rsd = sb("rsd", [C2, 512])
        out = sb("out", [C, 2, R * PW])
        dwv = sb("dwv", [C2, 10])
        hv = sb("hv", [C2, 2, (R + 2) * PW])
        v = sb("v", [C2, 2, 512])
        VT, FIRST = 9, 4
        bq = [pb("q0"), pb("q1")]
        bf = [pb("f0"), pb("f1")]
        bv, bp = pb("bv"), pb("bp")
        bx, by = pb("x"), pb("y")
        names = ["consts", "chain", "lb_ready", "w_psum", "w_ready", "bordered",
                 "qk_done", "qk_out", "v_done", "f_done", "k_out", "z_done", "inv_done", "inv_out", "cen_done",
                 "sq_out", "var_done", "sd_out", "rsd_out", "cn_out", "ga_out", "t_out", "proj_done", "res_out",
                 "top_done", "top_out", "v_out", "v_tap"]
        s = {n: sem(n) for n in names}
        loaded = [sem(f"loaded{k}") for k in range(2)]
        stored = [sem(f"stored{k}") for k in range(2)]
        block = ctx.enter_context(nc.Block())

        def turns(eng, b, turn):
            for i in (0, None):
                with ExitStack() as loop:
                    if i is None:
                        i = loop.enter_context(eng.Fori(1, NBLK // 2))
                    for k in range(2):
                        for n in range(GROUPS):
                            old = min(k * GROUPS + n, 2) if isinstance(i, int) else 2
                            turn((b * NBLK + 2 * i + k) * GROUPS + n, i, k, n, old)

        @block.sync
        def _(sp):
            cs = ((win, "l2_w"), (dw, "l2_dw"), (bdw, "l2_bdw"), (a, "k_a"), (cinv, "k_c"), (mean, "k_mean"),
                  (center, "k_center"), (dwv, "l2_dwv"), (gb, "l2_gb"), (bout, "l2_bout"), (wout, "l2_wout"))
            assert len(cs) == 11
            for dst, src in cs:
                sp.dma_start(dst[:], D[src]).then_inc(s["consts"], 16)
            with sp.Fori(0, NB) as b:
                with sp.Fori(0, NBLK // 2) as i:
                    for k in range(2):
                        sp.wait_ge(s["res_out"], (b * NBLK + 2 * i + k + 1) * GROUPS)
                        load_block(nc, sp, D, "x2", b, (2 * i + k) * R, T, k, R + 1, loaded[k])

        @block.tensor
        def _(pe):
            def convolve_qk(g, tile, n, half):
                pe.wait_ge(s["qk_out"], g * 2 + half + 1)
                for m2 in range(2):
                    r, x0 = 2 * n + half, 128 * m2
                    for m in range(6):
                        last = nc.tensor.matmul(bq[half][:, m2 * QK:(m2 + 1) * QK],
                                                tile[:, r + m // 3, x0 + m % 3:x0 + m % 3 + 128], w[:, m, 0:QK],
                                                start=(m == 0), stop=(m == 5))
                last.then_inc(s["qk_done"], 1)

            def spectrum(g, m2):
                if m2 % 2 == 0:
                    pe.wait_ge(s["qk_out"], 2 + g * 2 + m2 // 2 + 1)
                pe.wait_ge(s["z_done"], g * 4 + m2 + 1)
                for p in range(2):
                    last = nc.tensor.matmul(bf[m2 % 2][0:SLOTS, p * QK:(p + 1) * QK], a[:, p, 0:SLOTS],
                                            qk[:, m2 // 2, (m2 % 2) * QK:(m2 % 2 + 1) * QK], start=True, stop=True)
                last.then_inc(s["f_done"], 1)

            def hidden_v(g, tile, n):
                pe.wait_ge(s["v_out"], 1 + g)
                nc.tensor.matmul(bv[0:C2, :], w[:, 1, QK:C6], tile[:, 2 * n + 1:2 * n + 3, 1:W + 1],
                                 start=True, stop=True).then_inc(s["v_done"], 1)

            def inverse(g):
                pe.wait_ge(s["sd_out"], 1 + g)
                pe.wait_ge(s["z_done"], 2 + g * 4 + 4)
                for m in range(8):
                    last = nc.tensor.matmul(bx[0:C2, m * 64:(m + 1) * 64],
                                            z[:, m // 2, (m % 2) * C2:(m % 2 + 1) * C2], cinv[:], start=True, stop=True)
                last.then_inc(s["inv_done"], 1)

            def centred(g):
                pe.wait_ge(s["cn_out"], 1 + g)
                pe.wait_ge(s["inv_out"], g + 1)
                nc.tensor.matmul(by[0:C2, :], center[:], mixed[:], start=True, stop=True).then_inc(s["cen_done"], 1)

            def variance(g):
                pe.wait_ge(s["sq_out"], g + 1)
                nc.tensor.matmul(bx[0:C2, :], mean[:], sq[:], start=True, stop=True).then_inc(s["var_done"], 1)

            def project(g):
                pe.wait_ge(s["t_out"], 2 + g + 1)
                pe.wait_ge(s["res_out"], 2 * GROUPS + g)
                nc.tensor.matmul(bp[0:C, :], wout[:], t[:], start=True, stop=True).then_inc(s["proj_done"], 1)

            with pe.Fori(0, NB) as b:
                pe.wait_ge(s["lb_ready"], b + 1)
                nc.tensor.matmul(bf[0][0:K2, 0:C6], lb[:], win[:], start=True, stop=True).then_inc(s["w_psum"], 1)

                def turn(g, i, k, n, old):
                    if n == 0:
                        if k == 0:
                            pe.wait_ge(s["w_ready"], b + 1)
                        pe.wait_ge(loaded[k], (b * (NBLK // 2) + i + 1) * 48)
                    tile = T[:, k, :].rearrange("p (r w) -> p r w", w=PW)
                    if not old:
                        pe.wait_ge(s["res_out"], 2 * GROUPS + g)
                        nc.tensor.matmul(bp[0:C2, :], w[:, 0, QK:C6], tile[:, 0:2, 1:W + 1], start=True, stop=True)\
                            .then_inc(s["top_done"], 1)
                    convolve_qk(g, tile, n, 0)
                    if old:
                        inverse(g - 1)
                    hidden_v(g, tile, n)
                    if old:
                        centred(g - 1)
                    convolve_qk(g, tile, n, 1)
                    if old:
                        variance(g - 1)
                    if old > 1:
                        project(g - 2)
                    for m2 in range(4):
                        spectrum(g, m2)
                turns(pe, b, turn)
                g = (b + 1) * (NBLK * GROUPS) - 1
                inverse(g)
                centred(g)
                variance(g)
                project(g - 1)
                project(g)

        @block.scalar
        def _(act):
            def read_qk(g, half):
                act.wait_ge(s["qk_done"], g * 2 + half + 1)
                if half == 0:
                    act.wait_ge(s["f_done"], 1 + g * 4)
                nc.scalar.activation(qk[:, half, :], bq[half][:, 0:2 * QK], ACT.Copy).then_inc(s["qk_out"], 1)

            def read_k(g, m2):
                act.wait_ge(s["f_done"], 1 + g * 4 + m2 + 1)
                act.wait_ge(s["z_done"], g * 4 + m2 + 1)
                nc.scalar.activation(ks[:, m2 % 2, :].rearrange("p (h o) -> p h o", h=2),
                                     bf[m2 % 2][0:SLOTS, 0:2 * QK].rearrange("p (h o) -> p h o", h=2)[:, :, C2:QK],
                                     ACT.Copy).then_inc(s["k_out"], 1)

            def read_mixed(g):
                act.wait_ge(s["inv_done"], 1 + g + 1)
                nc.scalar.activation(mixed[:], bx[0:C2, :], ACT.Copy).then_inc(s["inv_out"], 1)

            def square(g):
                act.wait_ge(s["cen_done"], g + 1)
                nc.scalar.activation(sq[:], by[0:C2, :], ACT.Square).then_inc(s["sq_out"], 1)

            def deviation(g):
                act.wait_ge(s["var_done"], g + 1)
                act.wait_ge(s["cn_out"], 1 + g)
                nc.scalar.activation(sd[:], bx[0:C2, :], ACT.Sqrt, bias=eps[:, 0:1]).then_inc(s["sd_out"], 1)

            def affine(g):
                act.wait_ge(s["cn_out"], 1 + g + 1)
                act.wait_ge(s["t_out"], 2 + g)
                nc.scalar.activation(ga[:], cn[:], ACT.Identity, scale=gb[:, 0:1], bias=gb[:, 1:2])\
                    .then_inc(s["ga_out"], 1)

            def store(b, block, k):
                act.wait_ge(s["res_out"], 2 * GROUPS + (b * NBLK + block + 1) * GROUPS)
                dst = D["x3"][bass.ds(b, 1), :, bass.ds(block * R + 1, R), :]
                act.dma_start(rows2(dst.rearrange("a c h w -> (a c) h w")), out[:, k, :]).then_inc(stored[k], 16)

            with act.Fori(0, NB) as b:
                def turn(g, i, k, n, old):
                    def window(k):
                        return hv[:, k, :].rearrange("p (r w) -> p r w", w=PW)

                    if not old:
                        act.wait_ge(s["top_done"], b + 1)
                        nc.scalar.activation(window(k)[:, 0:2, 1:W + 1], bp[0:C2, :].rearrange("p (r w) -> p r w", r=2),
                                             ACT.Copy).then_inc(s["top_out"], 1)
                    read_qk(g, 0)
                    if old:
                        read_mixed(g - 1)
                    if old > 1:
                        affine(g - 2)
                    if n == 2 and old > 1 and not (k == 0 and isinstance(i, int)):
                        store(b, 2 * i + k - 1, 1 - k)
                    act.wait_ge(s["v_done"], g + 1)
                    rows = bv[0:C2, :].rearrange("p (r w) -> p r w", r=2)
                    if n == GROUPS - 1:
                        nc.scalar.activation(window(1 - k)[:, 0:2, 1:W + 1], rows, ACT.Copy)
                    nc.scalar.activation(window(k)[:, 2 * n + 2:2 * n + 4, 1:W + 1], rows, ACT.Copy)\
                        .then_inc(s["v_out"], 1)
                    if old:
                        square(g - 1)
                    read_qk(g, 1)
                    if old:
                        deviation(g - 1)
                    for m2 in range(4):
                        read_k(g, m2)
                turns(act, b, turn)
                g = (b + 1) * (NBLK * GROUPS) - 1
                read_mixed(g)
                affine(g - 1)
                square(g)
                deviation(g)
                affine(g)
                store(b, NBLK - 1, 1)
            for k in range(2):
                act.wait_ge(stored[k], 16 + 16 * NB * (NBLK // 2))

        @block.vector
        def _(dve):
            nc.vector.memset(out[:], 0.0).then_inc(s["bordered"], 1)
            nc.vector.memset(eps[:], GROUP_EPS).then_inc(s["bordered"], 1)
            nc.vector.memset(hv[:], 0.0).then_inc(s["bordered"], 1)
            for n in ("f_done", "cn_out", "inv_done", "ga_out", "proj_done", "sd_out", "v_out"):
                dve.sem_inc(s[n], 1)
            dve.sem_inc(s["qk_out"], 2)
            dve.sem_inc(s["z_done"], 2)
            dve.sem_inc(s["t_out"], 2)
            dve.sem_inc(s["res_out"], 2 * GROUPS)
            for k in range(2):
                dve.sem_inc(stored[k], 16)
            dve.wait_ge(s["bordered"], 3)
            dve.wait_ge(s["consts"], 176)
            with dve.Fori(0, NB) as b:
                norm_weights(nc, dve, S, b, tmp, lb, s["lb_ready"], s["chain"], 2 * b + 1)
                dve.wait_ge(s["w_psum"], b + 1)
                for m in range(6):
                    last = nc.vector.tensor_tensor(w[:, m, :], bf[0][0:K2, 0:C6], dw[:, m, :], ALU.mult)
                last.then_inc(s["chain"], 1)
                dve.wait_ge(s["chain"], 2 * b + 2)
                nc.vector.tensor_tensor(w[:, 1, :], w[:, 1, :], bdw[:], ALU.add).then_inc(s["w_ready"], 1)

                def products(g, m2):
                    if m2 == 0:
                        dve.wait_ge(s["inv_done"], 1 + g)
                    dve.wait_ge(s["k_out"], g * 4 + m2 + 1)
                    nc.vector.tensor_tensor(
                        z[:, m2, :].rearrange("p (h o) -> p h o", h=2),
                        bf[m2 % 2][0:SLOTS, 0:2 * QK].rearrange("p (h o) -> p h o", h=2)[:, :, 0:C2],
                        ks[:, m2 % 2, :].rearrange("p (h o) -> p h o", h=2), ALU.mult).then_inc(s["z_done"], 1)

                def taps(g, k, n, some):
                    rows = hv[:, k, :].rearrange("p (r w) -> p r w", w=PW)
                    o = v[:, n % 2, :].rearrange("p (r w) -> p r w", r=2)
                    for m in some:
                        x = rows[:, 2 * n + m // 3:2 * n + m // 3 + 2, m % 3:m % 3 + W]
                        if m == 0:
                            if n == 0:
                                dve.wait_ge(s["top_out"], b + 1)
                            dve.wait_ge(s["v_out"], 1 + g + 1)
                            last = nc.vector.tensor_scalar(o, x, dwv[:, 0:1], dwv[:, 9:10], ALU.mult, ALU.add)
                        else:
                            dve.wait_ge(s["v_tap"], g * VT + m)
                            last = nc.vector.scalar_tensor_tensor(out=o, in0=x, scalar=dwv[:, m:m + 1], in1=o,
                                                                  op0=ALU.mult, op1=ALU.add)
                        last.then_inc(s["v_tap"], 1)

                def normalise(g):
                    dve.wait_ge(s["sd_out"], 1 + g + 1)
                    dve.wait_ge(s["ga_out"], 1 + g)
                    nc.vector.reciprocal(rsd[:], sd[:]).then_inc(s["rsd_out"], 1)
                    dve.wait_ge(s["rsd_out"], g + 1)
                    nc.vector.tensor_tensor(cn[:], by[0:C2, :], rsd[:], ALU.mult).then_inc(s["cn_out"], 1)

                def times_v(g, n):
                    dve.wait_ge(s["ga_out"], 1 + g + 1)
                    dve.wait_ge(s["v_tap"], (g + 1) * VT)
                    dve.wait_ge(s["proj_done"], 1 + g)
                    nc.vector.tensor_tensor(t[:], v[:, n % 2, :], ga[:], ALU.mult).then_inc(s["t_out"], 1)

                def residual(g, i, k, n):
                    dve.wait_ge(s["proj_done"], 1 + g + 1)
                    if n == 0:
                        dve.wait_ge(stored[k], (b * (NBLK // 2) + i + 1) * 16)
                    o = out[:, k, :].rearrange("p (r w) -> p r w", w=PW)
                    tile = T[:, k, :].rearrange("p (r w) -> p r w", w=PW)
                    nc.vector.scalar_tensor_tensor(
                        out=o[:, 2 * n:2 * n + 2, 1:W + 1],
                        in0=bp[0:C, :].rearrange("p (r w) -> p r w", r=2), scalar=bout[:, 0:1],
                        in1=tile[0:C, 2 * n + 1:2 * n + 3, 1:W + 1], op0=ALU.add, op1=ALU.add)\
                        .then_inc(s["res_out"], 1)

                def turn(g, i, k, n, old):
                    before = (k if n > 0 else 1 - k, (n - 1) % GROUPS)
                    if old:
                        taps(g - 1, *before, range(FIRST, FIRST + 3))
                    if old > 1:
                        times_v(g - 2, n)
                    if old:
                        taps(g - 1, *before, range(FIRST + 3, VT))
                    taps(g, k, n, range(FIRST))
                    for m2 in range(4):
                        products(g, m2)
                    if old > 1:
                        residual(g - 2, i, k if n > 1 else 1 - k, (n - 2) % GROUPS)
                    if old:
                        normalise(g - 1)
                turns(dve, b, turn)
                g = (b + 1) * (NBLK * GROUPS) - 1
                taps(g, 1, GROUPS - 1, range(FIRST, VT))
                times_v(g - 1, GROUPS - 2)
                residual(g - 1, None, 1, GROUPS - 2)
                normalise(g)
                times_v(g, GROUPS - 1)
                residual(g, None, 1, GROUPS - 1)


def stage_l3(nc, D, S, NB):
    NB3 = NBLK + 1
    SL = 3
    GT = 4
    GROUPS = 2 * R // GT
    WIN = R + 2
    ON_PE = (3, 2, 3)
    UNITS = 6
    NT = [9 - ON_PE[u % 3] for u in range(UNITS)]
    BEFORE = [sum(NT[:u]) for u in range(UNITS + 1)]
    HR = R // 2
    HN = HR * W
    TILES_OF = ((0, 1, 2), (3, 4, 5), (6, 7, 8), (9, 10, 11), (12, 13, 14), (15,))
    PROJECT_AT = (1, 2, 4, 5)
    NP3 = len(PROJECT_AT)
    with ExitStack() as ctx:
        def sb(name, shape):
            return ctx.enter_context(nc.sbuf_tensor(f"l3_{name}", shape, F32))

        def pb(name):
            return ctx.enter_context(nc.psum_tensor(f"l3_{name}", [128, 512], F32))

        def sem(name):
            return ctx.enter_context(nc.semaphore(f"l3_{name}"))
        T = sb("T", [C + 1, SL, (R + 1) * PW])
        xp = sb("xp", [C + 1, 2, GT * 128])
        win, ln, lt = sb("win", [C, C6]), sb("ln", [C + 1, B, C]), sb("lt", [C, B, C + 1])
        ma, mb, f, fi = sb("ma", [128, C6]), sb("mb", [128, C6]), sb("f", [128, 128]), sb("fi", [128, 128])
        dw, wout = sb("dw", [PP, 3, 9]), sb("wout", [C, 3, C2])
        diag = sb("diag", [PP, 3, max(ON_PE), PP])
        xt, xf = sb("xt", [128, 2, GT * C]), sb("xf", [C, 2, GT * 128])
        ym = sb("ym", [128, 2, GT, 3, 2 * HI])
        rows = sb("rows", [PP, 3, SL, WIN * PW])
        acc = sb("acc", [PP, 2, HN])
        gl, gate = sb("gl", [PP, HN]), sb("gate", [C, 2, 3, HN])
        out = sb("out", [C, 2, HN])
        bt, by, bi, bo = pb("t"), [pb("y0"), pb("y1")], [pb("i0"), pb("i1")], pb("o")
        bd = ctx.enter_context(nc.psum_tensor("l3_d", [128, 1024], F32))
        names = ["consts", "ready", "prep", "ln_psum", "ln_ready", "xt_done", "xt_out", "xf_done", "xf_out",
                 "y_done", "ym_out", "i_done", "rows_out", "shifted", "d_done", "tap", "gl_out", "gate_out",
                 "o_done", "res_out", "xp_out", "spreading", "gathering"]
        s = {n: sem(n) for n in names}
        loaded = [sem(f"loaded{k}") for k in range(SL)]
        stored = sem("stored")
        FREE = {"ym_out": 2, "rows_out": 2, "tap": NT[UNITS - 1], "res_out": 3, "y_done": GT + 1, "i_done": 4,
                "gate_out": 1, "xt_done": 2, "xf_out": 1, "shifted": 1, "o_done": 1, "stored": 16}
        block = ctx.enter_context(nc.Block())

        def window(j, k):
            return rows[:, j, k, :].rearrange("p (r w) -> p r w", w=PW)

        def tap_rows(j, k, r, n, t):
            return window(j, k)[:, r + t // 3:r + t // 3 + n, t % 3:t % 3 + W]

        def turns(eng, turn):
            with eng.Fori(0, NB) as b:
                with eng.Fori(0, NB3 // SL) as i:
                    for k in range(SL):
                        turn(b, b * NB3 + SL * i + k, k, b * (NB3 // SL) + i)
            turn(None, NB * NB3, 0, None)
        LAST = NB * NB3

        def steps(lap, u, second):
            for at, m in enumerate(TILES_OF[u]) if lap is not None else ():
                if (at == 2) != second:
                    continue
                g = m // GT
                if m == 0:
                    yield "spectrum", 0
                yield "channels", m
                if m % GT == 0 and g < GROUPS - 1:
                    yield "spread", g + 1
                if m % GT == 1 and g > 0:
                    yield "inverse", g - 1
                if m % GT == 2 and g < GROUPS - 1:
                    yield "spectrum", g + 1
                if m == 2 * R - 1:
                    yield "inverse", g

        @block.sync
        def _(sp):
            cs = ((win, "l3_win"), (ma, "l3_ma"), (mb, "l3_mb"), (f, "k_f"), (fi, "k_g"), (dw, "l3_dw"),
                  (wout, "l3_wout"))
            for dst, src in cs:
                sp.dma_start(dst[:], D[src]).then_inc(s["consts"], 16)
            sp.wait_ge(s["ready"], 7)

            def store(n):
                sp.wait_ge(s["res_out"], FREE["res_out"] + NP3 * n + 2)
                sp.dma_start(D["out"][bass.ds(n, 1)].rearrange("a c n -> (a c) n"), out[:].rearrange("p h n -> p (h n)"))\
                  .then_inc(stored, 16)
            with sp.Fori(0, NB) as b:
                with sp.Fori(0, NB3 // SL) as i:
                    for k in range(SL):
                        n, blk = b * NB3 + SL * i + k, SL * i + k
                        sp.wait_ge(s["res_out"], FREE["res_out"] + NP3 * n - 2)
                        src = D["x3"][bass.ds(b, 1), :, bass.ds(blk * R, R + 1), :]
                        sp.dma_start(T[0:C, k, :], rows2(src.rearrange("a c h w -> (a c) h w"))).then_inc(loaded[k], 16)
                        sp.dma_start(T[C:C + 1, k, :], rows2(D["k_ones"][0:1, bass.ds(blk * R, R + 1), :]))\
                          .then_inc(loaded[k], 16)
                        store(n)
            store(LAST)
            store(LAST + 1)
            sp.wait_ge(stored, FREE["stored"] + 16 * (LAST + 2))

        @block.gpsimd
        def _(pool):
            def turn(b, n, k, lap):
                for g in range(GROUPS) if lap is not None else ():
                    if g == 0:
                        pool.wait_ge(loaded[k], (lap + 1) * 32)
                    pool.wait_ge(s["xt_done"], n * GROUPS + g + 1)
                    pool.sem_inc(s["gathering"], 1)
                    tile = T[:, k, :].rearrange("p (r w) -> p r w", w=PW)
                    x0 = 1 + g * GT * 16
                    nc.gpsimd.tensor_copy(xp[:, g % 2, :].rearrange("p (t r x) -> p t r x", t=GT, r=R),
                                          tile[:, 1:R + 1, x0:x0 + GT * 16].rearrange("p r (t x) -> p t r x", t=GT))\
                        .then_inc(s["xp_out"], 1)
            pool.wait_ge(s["ready"], 7)
            turns(pool, turn)

        @block.tensor
        def _(pe):
            def spread(b, n, k, g):
                G = n * GROUPS + g
                pe.wait_ge(s["xf_out"], 1 + G)
                pe.wait_ge(s["xp_out"], G + 1)
                pe.sem_inc(s["spreading"], 1)
                for t in range(GT):
                    last = nc.tensor.matmul(bt[:, t * C:(t + 1) * C], xp[:, g % 2, t * 128:(t + 1) * 128],
                                            ln[:, bass.ds(b, 1), :].rearrange("p a c -> p (a c)"),
                                            start=True, stop=True)
                last.then_inc(s["xt_done"], 1)

            def spectrum(n, g):
                G = n * GROUPS + g
                pe.wait_ge(s["xt_out"], G + 1)
                for t in range(GT):
                    last = nc.tensor.matmul(bt[0:C, t * 128:(t + 1) * 128], xt[:, g % 2, t * C:(t + 1) * C], f[:],
                                            start=True, stop=True)
                last.then_inc(s["xf_done"], 1)

            def channels(n, m):
                if m % GT == 0:
                    pe.wait_ge(s["xf_out"], 1 + n * GROUPS + m // GT + 1)
                pe.wait_ge(s["ym_out"], n * 2 * R + m + 1)
                t = m % GT
                nc.tensor.matmul(by[m % 2][:, 0:C6], xf[:, (m // GT) % 2, t * 128:(t + 1) * 128], win[:],
                                 start=True, stop=True).then_inc(s["y_done"], 1)

            def inverse(n, g):
                pe.wait_ge(s["ym_out"], FREE["ym_out"] + (n * GROUPS + g + 1) * GT)
                for j in range(3):
                    pe.wait_ge(s["rows_out"], (n * GROUPS + g) * 3 + j + 1)
                    for t in range(GT):
                        last = nc.tensor.matmul(bi[(3 * g + j) % 2][0:PP, t * 128:(t + 1) * 128],
                                                ym[:, g % 2, t, j, 0:PP], fi[:], start=True, stop=True)
                    last.then_inc(s["i_done"], 1)

            def depthwise(n, k, u):
                j, h = u % 3, u // 3
                if u == 0:
                    pe.wait_ge(s["rows_out"], FREE["rows_out"] + n * GROUPS * 3)
                    pe.wait_ge(s["shifted"], 1 + n)
                pe.wait_ge(s["tap"], FREE["tap"] + n * BEFORE[UNITS] + (BEFORE[u - 1] if u else -NT[UNITS - 1]) + 1)
                for q in range(2):
                    for t in range(ON_PE[j]):
                        last = nc.tensor.matmul(bd[0:PP, q * 512:(q + 1) * 512], diag[:, j, t, :],
                                                tap_rows(j, (k - 1) % SL, h * HR + 2 * q, 2, t),
                                                start=(t == 0), stop=(t == ON_PE[j] - 1))
                last.then_inc(s["d_done"], 1)

            def project(n, part):
                h, q = 1 - part // 2, part % 2
                pe.wait_ge(s["gate_out"], FREE["gate_out"] + 1 + n * UNITS + (0 if h else 3))
                pe.wait_ge(s["res_out"], FREE["res_out"] + n * NP3 + part)
                for j in range(3):
                    last = nc.tensor.matmul(bo[0:C2, :], wout[:, j, :], gate[:, h, j, q * 512:(q + 1) * 512],
                                            start=(j == 0), stop=(j == 2))
                last.then_inc(s["o_done"], 1)

            def turn(b, n, k, lap):
                work = {"spread": lambda g: spread(b, n, k, g), "spectrum": lambda g: spectrum(n, g),
                        "channels": lambda m: channels(n, m), "inverse": lambda g: inverse(n, g)}
                if lap is not None:
                    spread(b, n, k, 0)
                depthwise(n, k, 0)
                for u in range(UNITS):
                    for name, m in steps(lap, u, False):
                        work[name](m)
                    if u < UNITS - 1:
                        depthwise(n, k, u + 1)
                    for name, m in steps(lap, u, True):
                        work[name](m)
                    if u in PROJECT_AT:
                        project(n, PROJECT_AT.index(u))

            pe.wait_ge(s["prep"], 1)
            for b in range(NB):
                last = nc.tensor.matmul(bt[0:C + 1, b * C:(b + 1) * C], lt[:, b, :], S["k_ident"][0:C, 0:C],
                                        start=True, stop=True)
            last.then_inc(s["ln_psum"], 1)
            pe.wait_ge(s["ln_ready"], 1)
            pe.wait_ge(s["consts"], 112)
            turns(pe, turn)
            for part in range(2):
                project(LAST + 1, part)

        @block.scalar
        def _(act):
            def gelu(n, u):
                act.wait_ge(s["tap"], FREE["tap"] + n * BEFORE[UNITS] + BEFORE[u])
                act.wait_ge(s["gate_out"], FREE["gate_out"] + n * UNITS + u)
                nc.scalar.activation(gl[HI:HI + C, :], acc[0:C, (u - 1) % 2, :], ACT.Gelu).then_inc(s["gl_out"], 1)

            def turn(b, n, k, lap):
                def read_pixels(g):
                    act.wait_ge(s["xt_done"], FREE["xt_done"] + n * GROUPS + g + 1)
                    nc.scalar.activation(xt[:, g % 2, :], bt[:, 0:GT * C], ACT.Copy).then_inc(s["xt_out"], 1)

                def read_spectra(g):
                    act.wait_ge(s["xf_done"], n * GROUPS + g + 1)
                    act.wait_ge(s["y_done"], 1 + (n * GROUPS + g) * GT)
                    nc.scalar.activation(xf[:, g % 2, :], bt[0:C, :], ACT.Copy).then_inc(s["xf_out"], 1)

                def read_rows(g):
                    for j in range(3):
                        act.wait_ge(s["i_done"], FREE["i_done"] + (n * GROUPS + g) * 3 + j + 1)
                        x0 = 1 + g * GT * 16
                        nc.scalar.activation(
                            window(j, k)[:, 2:WIN, x0:x0 + GT * 16].rearrange("p r (t x) -> p t r x", t=GT),
                            bi[(3 * g + j) % 2][0:PP, :].rearrange("p (t r x) -> p t r x", t=GT, r=R),
                            ACT.Copy).then_inc(s["rows_out"], 1)
                work = {"spread": read_pixels, "spectrum": read_spectra, "inverse": read_rows,
                        "channels": lambda m: None}
                if lap is not None:
                    read_pixels(0)
                    act.wait_ge(s["rows_out"], FREE["rows_out"] + n * GROUPS * 3)
                    nc.scalar.activation(rows[:, :, k, 0:2 * PW], rows[:, :, (k - 1) % SL, R * PW:WIN * PW], ACT.Copy)\
                        .then_inc(s["shifted"], 1)
                for u in range(UNITS):
                    for name, m in steps(lap, u, False):
                        work[name](m)
                    gelu(n, u)
                    for name, m in steps(lap, u, True):
                        work[name](m)
            act.wait_ge(s["ready"], 7)
            turns(act, turn)
            gelu(LAST + 1, 0)

        @block.vector
        def _(dve):
            nc.vector.memset(rows[:], 0.0).then_inc(s["ready"], 1)
            nc.vector.memset(ym[:], 0.0).then_inc(s["ready"], 1)
            nc.vector.memset(T[:], 0.0).then_inc(s["ready"], 1)
            nc.vector.memset(acc[:], 0.0).then_inc(s["ready"], 1)
            nc.vector.memset(gl[:], 0.0).then_inc(s["ready"], 1)
            nc.vector.memset(out[:], 0.0).then_inc(s["ready"], 1)
            nc.vector.memset(gate[:], 0.0).then_inc(s["ready"], 1)
            dve.wait_ge(s["ready"], 7)
            for name, n in FREE.items():
                dve.sem_inc(stored if name == "stored" else s[name], n)
            dve.wait_ge(s["consts"], 112)
            for b in range(NB):
                nc.vector.tensor_scalar(lt[:, b, 0:C], S["k_ident"][0:C, 0:C], S["gn"][0:C, b, 0:1], None, ALU.mult)
                last = nc.vector.tensor_copy(lt[:, b, C:C + 1], S["gn"][0:C, b, 1:2])
            last.then_inc(s["prep"], 1)
            for j in range(3):
                for t in range(ON_PE[j]):
                    nc.vector.tensor_scalar(diag[:, j, t, :], S["k_ident"][0:PP, 0:PP], dw[:, j, t:t + 1], None,
                                            ALU.mult)
            nc.vector.tensor_tensor(ma[:], ma[:], mb[:], ALU.add).then_inc(s["prep"], 1)
            dve.wait_ge(s["prep"], 2)
            nc.vector.tensor_scalar(ma[:], ma[:], 0.5, None, ALU.mult).then_inc(s["prep"], 1)
            dve.wait_ge(s["ln_psum"], 1)
            nc.vector.tensor_copy(ln[:, 0:NB, :].rearrange("p b c -> p (b c)"), bt[0:C + 1, 0:NB * C])\
                .then_inc(s["ln_ready"], 1)
            dve.wait_ge(s["prep"], 3)

            def make_gate(n, u):
                h, j = (u - 1) % UNITS // 3, (u - 1) % 3
                dve.wait_ge(s["gl_out"], n * UNITS + u + 1)
                if j == 0:
                    dve.wait_ge(s["o_done"], FREE["o_done"] + n * NP3 + (2 if h else 0))
                nc.vector.tensor_tensor(gate[:, h, j, :], gl[HI:HI + C, :], acc[HI:HI + C, (u - 1) % 2, :], ALU.mult)\
                    .then_inc(s["gate_out"], 1)

            def residual(n, k, part):
                h, q = 1 - part // 2, part % 2
                dve.wait_ge(s["o_done"], FREE["o_done"] + n * NP3 + part + 1)
                if part == 2:
                    dve.wait_ge(stored, 16 * (n + 2))
                r = h * HR + 2 * q
                tile = T[0:C, (k - 1 - h) % SL, :].rearrange("p (r w) -> p r w", w=PW)
                nc.vector.tensor_tensor(
                    out[:, h, q * 512:(q + 1) * 512].rearrange("p (r w) -> p r w", w=W),
                    bo[0:C, :].rearrange("p (r w) -> p r w", w=W), tile[:, r:r + 2, 1:W + 1], ALU.add)\
                    .then_inc(s["res_out"], 1)

            def turn(b, n, k, lap):
                def mask(m):
                    g, t = m // GT, m % GT
                    dve.wait_ge(s["y_done"], FREE["y_done"] + n * 2 * R + m + 1)
                    if t == 0:
                        dve.wait_ge(s["i_done"], 1 + (n * GROUPS + g) * 3)
                    nc.vector.tensor_tensor(
                        ym[:, g % 2, t].rearrange("p j (h c) -> p j h c", h=2)[:, :, :, 0:C],
                        by[m % 2][:, 0:C6].rearrange("p (j h c) -> p j h c", j=3, h=2),
                        ma[:].rearrange("p (j h c) -> p j h c", j=3, h=2), ALU.mult).then_inc(s["ym_out"], 1)

                for u in range(UNITS):
                    U, h, j = n * UNITS + u, u // 3, u % 3
                    todo = list(TILES_OF[u]) if lap is not None else []
                    a = acc[:, u % 2, :].rearrange("p (r w) -> p r w", w=W)
                    for o, t in enumerate(range(ON_PE[j], 9)):
                        if o == 0:
                            dve.wait_ge(s["d_done"], U + 1)
                            dve.wait_ge(s["gate_out"], FREE["gate_out"] + U)
                        else:
                            dve.wait_ge(s["tap"], FREE["tap"] + n * BEFORE[UNITS] + BEFORE[u] + o)
                        nc.vector.scalar_tensor_tensor(
                            out=a, in0=tap_rows(j, (k - 1) % SL, h * HR, HR, t), scalar=dw[:, j, t:t + 1],
                            in1=a if o else bd[0:PP, :].rearrange("p (r w) -> p r w", w=W),
                            op0=ALU.mult, op1=ALU.add).then_inc(s["tap"], 1)
                        if todo and (o % 2 == 1 or u == UNITS - 1):
                            mask(todo.pop(0))
                        if o == 2 and u in (2, 3, 5):
                            residual(n, k, (2, 3, 5).index(u))
                        if o == 4:
                            make_gate(n, u)
                    if u == UNITS - 1:
                        residual(n, k, 3)
                    assert not todo
            turns(dve, turn)
            make_gate(LAST + 1, 0)
            for part in range(2):
                residual(LAST + 1, (LAST + 1) % SL, part)


OUTS = {"out": (B * (NBLK + 1) + 2, C, R * W)}
SCRATCH = {"x1": (B, C, PH, PW), "x2": (B, C, PH, PW), "x3": (B, C, PH3, PW), "u": (B, C, H, W)}


def build_program(nc, D, NB=B, stages="0A B1 2 3"):
    with ExitStack() as ctx:
        S = {n: ctx.enter_context(nc.sbuf_tensor(n, shape, F32)) for n, shape in (
            ("k_sel", [128, 128]), ("k_batch", [128, B]), ("k_onesrow", [128, 2]), ("k_ident", [128, 128]),
            ("k_e1", [C + 1, K2]), ("k_e2", [C + 1, K2]), ("gn", [128, B, 2]), ("gn1", [128, B]),
            ("mt", [C, B * C]))}
        stage_setup(nc, D, S)
        if "0" in stages:
            stage_stats(nc, D, S, "x_in", PH, "s0")
        if "A" in stages:
            stage_l0_attention(nc, D, S, NB)
        if "B" in stages:
            stage_l0_apply(nc, D, S, NB)
        if "1" in stages:
            stage_stats(nc, D, S, "x1", PH, "s1")
            stage_l1_sweeps(nc, D, S, NB)
        if "2" in stages:
            stage_stats(nc, D, S, "x2", PH, "s2")
            stage_l2(nc, D, S, NB)
        if "3" in stages:
            stage_stats(nc, D, S, "x3", PH3, "s3")
            stage_l3(nc, D, S, NB)


def by_image(blocks):
    v = blocks[2:].reshape(B, NBLK + 1, C, R, W).transpose(0, 2, 1, 3, 4).reshape(B, C, (NBLK + 1) * R, W)
    return np.ascontiguousarray(v[:, :, 1:H + 1, :])


def kernel(**inputs):
    import concourse.bacc as bacc
    from concourse.bass_utils import run_bass_kernel_spmd

    arrays = {**shape_constants(), **lay_out({n: np.asarray(a) for n, a in inputs.items()})}
    nc = bacc.Bacc("TRN2", target_bir_lowering=False, num_devices=1)
    D = {n: nc.dram_tensor(n + "_dram", a.shape, F32, kind="ExternalInput").ap() for n, a in arrays.items()}
    for n, shape in SCRATCH.items():
        D[n] = nc.dram_tensor(n + "_dram", shape, F32, kind="Internal").ap()
    D["out"] = nc.dram_tensor("out_dram", OUTS["out"], F32, kind="ExternalOutput").ap()
    build_program(nc, D)
    r = run_bass_kernel_spmd(nc, [{n + "_dram": np.ascontiguousarray(a) for n, a in arrays.items()}], core_ids=[0])
    return by_image(r.results[0]["out_dram"])
```
